# Optimizing a Trainium2 kernel written in Bass

```python
import numpy as np
import jax
import jax.numpy as jnp

def _softmax(x, axis=-1):
    return jax.nn.softmax(x, axis=axis)

def _gelu(x):
    return jax.nn.gelu(x, approximate=True)

def _silu(x):
    return jax.nn.silu(x)

def _sigmoid(x):
    return jax.nn.sigmoid(x)

def _layernorm(x, axis=-1, eps=1e-05):
    m = jnp.mean(x, axis=axis, keepdims=True)
    v = jnp.var(x, axis=axis, keepdims=True)
    return (x - m) / jnp.sqrt(v + eps)

def _scatter_add(tgt, idx, src, axis=0):
    return tgt.at[idx].add(src)

def _segment_sum(src, seg, n):
    return jax.ops.segment_sum(src, seg, n)
kernel_name = 'mk_flamingo_gated_d1_seqx_r4_b375f2'

def setup_inputs(seed: int=0):
    np.random.seed(seed)
    _w = jnp.asarray

    def _rec_inputs():
        import jax
        import jax.numpy as jnp
        _rk = jax.random.key(seed)
        x = 4.136e-05 + 0.9999 * jax.random.normal(jax.random.fold_in(_rk, 1), (4, 512, 512), jnp.float32)
        _lenS = 512 - jax.random.randint(jax.random.fold_in(_rk, 7), (4,), 0, max(1, 512 // 4) + 1, jnp.int32)
        _lenS2 = 512 - jax.random.randint(jax.random.fold_in(_rk, 8), (4,), 0, max(1, 512 // 4) + 1, jnp.int32)
        _ctx_1024P = jax.random.normal(jax.random.fold_in(_rk, 11), (4, 16, 256), jnp.float32)
        _ctx_1024c = jax.random.dirichlet(jax.random.fold_in(_rk, 511), 0.3 * jnp.ones((16,), jnp.float32), (4, 512))
        _ctx_1024t = jnp.einsum('bsk,bkd->bsd', _ctx_1024c, _ctx_1024P)
        _ctx_1024t = _ctx_1024t * jax.lax.rsqrt(jnp.mean(jnp.square(_ctx_1024t)) + 1e-12) * 0.953939
        ctx_1024 = -0.000292821 + 1.00034 * (_ctx_1024t + 0.3 * jax.random.normal(jax.random.fold_in(_rk, 611), (4, 512, 256), jnp.float32))
        _g = jax.random.normal(jax.random.fold_in(_rk, 9001), (2, 1), jnp.float32)
        _g = jnp.sign(_g) * jnp.maximum(jnp.abs(_g), 1.0) + (_g == 0) * 1.0
        g_xattn = _g[0]
        g_ffn = _g[1]
        return (x, ctx_1024, g_xattn, g_ffn)
    x, ctx_1024, g_xattn, g_ffn = _rec_inputs()

    def _L0_xattn_setup():
        import jax, jax.numpy as jnp
        import numpy as np
        import math
        B, L, DM = (2, 512, 256)
        DS, DC, EXP = (16, 4, 2)
        DI = EXP * DM
        DR = math.ceil(DM / 16)
        DT_MIN, DT_MAX, DT_FLOOR = (0.001, 0.1, 0.0001)

        def _ssm_forward(hidden_states, z, in_proj_w, conv_w, conv_b, x_proj_w, dt_proj_w, dt_proj_b, A_log, D):
            b = hidden_states.shape[0]
            x = jnp.einsum('ed,bld->bel', in_proj_w, hidden_states)
            xp = jnp.pad(x, ((0, 0), (0, 0), (DC - 1, 0)))
            xc = jax.lax.conv_general_dilated(xp, conv_w[:, None, :], window_strides=(1,), padding='VALID', dimension_numbers=('NCH', 'OIH', 'NCH'), feature_group_count=DI)
            u = jax.nn.silu(xc + conv_b[None, :, None])
            x_dbl = jnp.einsum('ke,bel->bkl', x_proj_w, u)
            dt_lo = x_dbl[:, :DR]
            Bm = x_dbl[:, DR:DR + DS]
            Cm = x_dbl[:, DR + DS:]
            delta = jax.nn.softplus(jnp.einsum('er,brl->bel', dt_proj_w, dt_lo) + dt_proj_b[None, :, None])
            A = -jnp.exp(A_log)

            def step(state, xs):
                d_t, B_t, C_t, u_t = xs
                dA = jnp.exp(d_t[..., None] * A)
                state = state * dA + (d_t * u_t)[..., None] * B_t[:, None, :]
                y_t = jnp.einsum('ben,bn->be', state, C_t)
                return (state, y_t)
            xs = (jnp.moveaxis(delta, -1, 0), jnp.moveaxis(Bm, -1, 0), jnp.moveaxis(Cm, -1, 0), jnp.moveaxis(u, -1, 0))
            state0 = jnp.zeros((b, DI, DS), delta.dtype)
            _, ys = jax.lax.scan(step, state0, xs)
            y = jnp.moveaxis(ys, 0, -1)
            y = y + D[None, :, None] * u
            y = y * jax.nn.silu(z)
            return jnp.swapaxes(y, 1, 2)
        key = jax.random.key(seed)
        ks = jax.random.split(key, 8)
        hidden_states = jax.random.normal(ks[0], (B, L, DM), jnp.float32)
        z = jax.random.normal(ks[1], (B, DI, L), jnp.float32)
        in_proj_w = jax.random.normal(ks[2], (DI, DM), jnp.float32) * DM ** (-0.5)
        conv_w = jax.random.normal(ks[3], (DI, DC), jnp.float32) * DC ** (-0.5)
        conv_b = jnp.zeros((DI,), jnp.float32)
        x_proj_w = jax.random.normal(ks[4], (DR + 2 * DS, DI), jnp.float32) * DI ** (-0.5)
        dt_std = DR ** (-0.5)
        dt_proj_w = jax.random.uniform(ks[5], (DI, DR), jnp.float32, -dt_std, dt_std)
        dt = jnp.exp(jax.random.uniform(ks[6], (DI,), jnp.float32) * (math.log(DT_MAX) - math.log(DT_MIN)) + math.log(DT_MIN))
        dt = jnp.clip(dt, DT_FLOOR)
        dt_proj_b = dt + jnp.log(-jnp.expm1(-dt))
        A_log = jnp.log(jnp.broadcast_to(jnp.arange(1, DS + 1, dtype=jnp.float32), (DI, DS)))
        D = jnp.ones((DI,), jnp.float32)
        return dict(hidden_states=hidden_states, z=z, in_proj_w=in_proj_w, conv_w=conv_w, conv_b=conv_b, x_proj_w=x_proj_w, dt_proj_w=dt_proj_w, dt_proj_b=dt_proj_b, A_log=A_log, D=D)
    _L0_xattn_all = _L0_xattn_setup()
    _L0_xattn_in = {k: v for k, v in _L0_xattn_all.items() if k in ('in_proj_w', 'conv_w', 'conv_b', 'x_proj_w', 'dt_proj_w', 'dt_proj_b', 'A_log', 'D')}
    del _L0_xattn_all

    def _L0_ffn_setup():
        import jax, jax.numpy as jnp
        import numpy as np
        NUM_ROUTED = 7
        TOP_K = 3
        D = 512
        H = 512
        B, S = (4, 512)

        def _expert_ffn(x, w1, wg, w2):
            return jax.nn.silu(x @ w1) * (x @ wg) @ w2
        key = jax.random.key(seed)
        ks = jax.random.split(key, 8)
        s = 0.02
        return {'x': jax.random.normal(ks[0], (B, S, D), jnp.float32), 'W1': jax.random.normal(ks[1], (NUM_ROUTED, D, H), jnp.float32) * s, 'Wg': jax.random.normal(ks[2], (NUM_ROUTED, D, H), jnp.float32) * s, 'W2': jax.random.normal(ks[3], (NUM_ROUTED, H, D), jnp.float32) * s, 'Ws1': jax.random.normal(ks[4], (D, H), jnp.float32) * s, 'Wsg': jax.random.normal(ks[5], (D, H), jnp.float32) * s, 'Ws2': jax.random.normal(ks[6], (H, D), jnp.float32) * s, 'gate_w': jax.random.normal(ks[7], (D, NUM_ROUTED), jnp.float32) * s, 'gate_b': jnp.zeros((NUM_ROUTED,), jnp.float32), 'biases': jnp.zeros((NUM_ROUTED,), jnp.float32)}
    _L0_ffn_all = _L0_ffn_setup()
    _L0_ffn_in = {k: v for k, v in _L0_ffn_all.items() if k in ('W1', 'Wg', 'W2', 'Ws1', 'Wsg', 'Ws2', 'gate_w', 'gate_b', 'biases')}
    del _L0_ffn_all
    return {'x': x, 'ctx_1024': ctx_1024, 'g_xattn': g_xattn, 'g_ffn': g_ffn, 'L0_xattn_in_proj_w': _L0_xattn_in['in_proj_w'], 'L0_xattn_conv_w': _L0_xattn_in['conv_w'], 'L0_xattn_conv_b': _L0_xattn_in['conv_b'], 'L0_xattn_x_proj_w': _L0_xattn_in['x_proj_w'], 'L0_xattn_dt_proj_w': _L0_xattn_in['dt_proj_w'], 'L0_xattn_dt_proj_b': _L0_xattn_in['dt_proj_b'], 'L0_xattn_A_log': _L0_xattn_in['A_log'], 'L0_xattn_D': _L0_xattn_in['D'], 'L0_ffn_W1': _L0_ffn_in['W1'], 'L0_ffn_Wg': _L0_ffn_in['Wg'], 'L0_ffn_W2': _L0_ffn_in['W2'], 'L0_ffn_Ws1': _L0_ffn_in['Ws1'], 'L0_ffn_Wsg': _L0_ffn_in['Wsg'], 'L0_ffn_Ws2': _L0_ffn_in['Ws2'], 'L0_ffn_gate_w': _L0_ffn_in['gate_w'], 'L0_ffn_gate_b': _L0_ffn_in['gate_b'], 'L0_ffn_biases': _L0_ffn_in['biases']}

def reference(x, ctx_1024, g_xattn, g_ffn, L0_xattn_in_proj_w, L0_xattn_conv_w, L0_xattn_conv_b, L0_xattn_x_proj_w, L0_xattn_dt_proj_w, L0_xattn_dt_proj_b, L0_xattn_A_log, L0_xattn_D, L0_ffn_W1, L0_ffn_Wg, L0_ffn_W2, L0_ffn_Ws1, L0_ffn_Wsg, L0_ffn_Ws2, L0_ffn_gate_w, L0_ffn_gate_b, L0_ffn_biases):
    import jax
    import jax.numpy as jnp

    def _L0_xattn_ref(hidden_states, z, in_proj_w, conv_w, conv_b, x_proj_w, dt_proj_w, dt_proj_b, A_log, D):
        import jax, jax.numpy as jnp
        import numpy as np
        import math
        B, L, DM = (2, 512, 256)
        DS, DC, EXP = (16, 4, 2)
        DI = EXP * DM
        DR = math.ceil(DM / 16)
        DT_MIN, DT_MAX, DT_FLOOR = (0.001, 0.1, 0.0001)

        def _ssm_forward(hidden_states, z, in_proj_w, conv_w, conv_b, x_proj_w, dt_proj_w, dt_proj_b, A_log, D):
            b = hidden_states.shape[0]
            x = jnp.einsum('ed,bld->bel', in_proj_w, hidden_states)
            xp = jnp.pad(x, ((0, 0), (0, 0), (DC - 1, 0)))
            xc = jax.lax.conv_general_dilated(xp, conv_w[:, None, :], window_strides=(1,), padding='VALID', dimension_numbers=('NCH', 'OIH', 'NCH'), feature_group_count=DI)
            u = jax.nn.silu(xc + conv_b[None, :, None])
            x_dbl = jnp.einsum('ke,bel->bkl', x_proj_w, u)
            dt_lo = x_dbl[:, :DR]
            Bm = x_dbl[:, DR:DR + DS]
            Cm = x_dbl[:, DR + DS:]
            delta = jax.nn.softplus(jnp.einsum('er,brl->bel', dt_proj_w, dt_lo) + dt_proj_b[None, :, None])
            A = -jnp.exp(A_log)

            def step(state, xs):
                d_t, B_t, C_t, u_t = xs
                dA = jnp.exp(d_t[..., None] * A)
                state = state * dA + (d_t * u_t)[..., None] * B_t[:, None, :]
                y_t = jnp.einsum('ben,bn->be', state, C_t)
                return (state, y_t)
            xs = (jnp.moveaxis(delta, -1, 0), jnp.moveaxis(Bm, -1, 0), jnp.moveaxis(Cm, -1, 0), jnp.moveaxis(u, -1, 0))
            state0 = jnp.zeros((b, DI, DS), delta.dtype)
            _, ys = jax.lax.scan(step, state0, xs)
            y = jnp.moveaxis(ys, 0, -1)
            y = y + D[None, :, None] * u
            y = y * jax.nn.silu(z)
            return jnp.swapaxes(y, 1, 2)
        return _ssm_forward(hidden_states, z, in_proj_w, conv_w, conv_b, x_proj_w, dt_proj_w, dt_proj_b, A_log, D)

    def _L0_ffn_ref(x, W1, Wg, W2, Ws1, Wsg, Ws2, gate_w, gate_b, biases):
        import jax, jax.numpy as jnp
        import numpy as np
        NUM_ROUTED = 7
        TOP_K = 3
        D = 512
        H = 512
        B, S = (4, 512)

        def _expert_ffn(x, w1, wg, w2):
            return jax.nn.silu(x @ w1) * (x @ wg) @ w2
        output = _expert_ffn(x, Ws1, Wsg, Ws2)
        gate_logits = x @ gate_w + gate_b
        gate_probas = jax.nn.softmax(gate_logits, axis=-1)
        biased_probas = gate_probas + biases
        _, topk_idxs = jax.lax.top_k(biased_probas, TOP_K)
        topk_probas = jnp.take_along_axis(gate_probas, topk_idxs, axis=-1)
        topk_probas = topk_probas / jnp.sum(topk_probas, axis=-1, keepdims=True)
        for e in range(NUM_ROUTED):
            w_e = jnp.sum(topk_probas * (topk_idxs == e), axis=-1)
            output = output + _expert_ffn(x, W1[e], Wg[e], W2[e]) * w_e[..., None]
        return output
    x = x + jnp.tanh(g_xattn[0]) * _L0_xattn_ref(ctx_1024, _layernorm(x, axis=-1), L0_xattn_in_proj_w, L0_xattn_conv_w, L0_xattn_conv_b, L0_xattn_x_proj_w, L0_xattn_dt_proj_w, L0_xattn_dt_proj_b, L0_xattn_A_log, L0_xattn_D)
    x = x + jnp.tanh(g_ffn[0]) * _L0_ffn_ref(_layernorm(x, axis=-1), L0_ffn_W1, L0_ffn_Wg, L0_ffn_W2, L0_ffn_Ws1, L0_ffn_Wsg, L0_ffn_Ws2, L0_ffn_gate_w, L0_ffn_gate_b, L0_ffn_biases)
    return x

_drawn_inputs = setup_inputs


def setup_inputs(seed=0):
    import zlib

    import numpy as np

    out = dict(_drawn_inputs(seed))
    spreads = {'L0_xattn_conv_b': (0.0, 0.279),
     'L0_xattn_D': (1.0, 0.2),
     'L0_ffn_gate_b': (0.0, 2.0),
     'L0_ffn_biases': (0.0, 1.404)}
    factors = {'L0_xattn_dt_proj_w': 6.627, 'L0_xattn_dt_proj_b': 2.923, 'L0_ffn_gate_w': 9.362}
    for name, (base, spread) in spreads.items():
        noise = np.random.default_rng([zlib.crc32(name.encode()), seed]).standard_normal(out[name].shape)
        drawn = base * np.exp(spread * noise) if base else spread * noise
        out[name] = jnp.asarray(drawn.astype(out[name].dtype))
    for name, factor in factors.items():
        out[name] = (out[name] * factor).astype(out[name].dtype)
    return out
```

```python
from contextlib import ExitStack

import concourse.bass as bass
from concourse import mybir

F32 = mybir.dt.float32
F32R = mybir.dt.float32r
ALU = mybir.AluOpType
ACT = mybir.ActivationFunctionType
AX_X = mybir.AxisListType.X

P = 128
NAMES = ["x", "ctxT", "g_xattn", "g_ffn", "in_wT", "conv_w", "conv_b", "xproj_wT", "dt_wT", "dt_b", "A_log", "D",
         "W1", "Wg", "W2", "Ws1", "Wsg", "Ws2", "gate_w", "gate_b", "biases", "ident", "earlier"]


def gated_block(nc, t, out):
    NB, L, DI = t["x"].shape
    DM = t["ctxT"].shape[1]
    NE = t["W1"].shape[0]
    DS = t["A_log"].shape[1]
    DC = t["conv_w"].shape[1]
    DR = t["dt_wT"].shape[0]
    XP = DR + 2 * DS
    TOP_K = 3
    EPS = 1e-5
    T = DI // P
    KM = DM // P
    STEPS = NE + 1
    assert L == DI and t["W1"].shape[1:] == (DI, DI)

    xd_dram = nc.dram_tensor("xd_scratch", (NB, 2 * DS, L), F32, kind="Internal").ap()

    with ExitStack() as ctx:
        def sb(name, shape, dt=F32):
            return ctx.enter_context(nc.sbuf_tensor(name, shape, dt))

        def sem(name):
            return ctx.enter_context(nc.semaphore(name))

        in_w = sb("in_w", [P, KM, DI])
        xproj_w = sb("xproj_w", [P, T, XP])
        dt_w = sb("dt_w", [DR, DI])
        conv_w = sb("conv_w", [P, T, DC])
        conv_b = sb("conv_b", [P, T])
        dt_b = sb("dt_b", [P, T])
        neg_A = sb("neg_A", [P, T, DS])
        half_D = sb("half_D", [P, T])
        gates = sb("gates", [P, 2])
        gate_tanh = sb("gate_tanh", [P, 2])
        half_tgf = sb("half_tgf", [P, 1])
        ones = sb("ones", [P, 1])
        minus_half = sb("minus_half", [P, T])
        gw_raw = sb("gw_raw", [P, T, NE + 1])
        gw_hi = sb("gw_hi", [P, T, NE + 1], F32R)
        gw_lo = sb("gw_lo", [P, T, NE + 1], F32R)
        gate_b = sb("gate_b", [P, NE])
        biases = sb("biases", [P, NE])
        ident = sb("ident", [P, P])
        earlier = sb("earlier", [P, NE, NE])

        ctxT = sb("ctxT", [P, KM, L])
        u = sb("u", [P, T, L])
        delta = sb("delta", [P, T, L])
        yacc = sb("yacc", [P, T, L])
        z2 = sb("z2", [P, T, L])
        xdbl = sb("xdbl", [XP, L])
        bc = [sb(f"bc{i}", [P, 2, L]) for i in range(2)]
        dA = [sb(f"dA{i}", [P, T, L]) for i in range(2)]
        st = [sb(f"st{i}", [P, T, L]) for i in range(2)]
        bn = sb("bn", [P, T, 6])
        mv = sb("mv", [P, T, 2])
        var_eps = sb("var_eps", [P, T])
        rstd = sb("rstd", [P, T])

        acc = sb("acc", [P, T, DI])
        x_hi = sb("x_hi", [P, T, L], F32R)
        x_lo = sb("x_lo", [P, T, L], F32R)
        h_tmp = [sb(f"h_tmp{i}", [P, L]) for i in range(2)]
        h_hi = sb("h_hi", [P, T, L], F32R)
        h_lo = sb("h_lo", [P, T, L], F32R)
        w_raw = [sb(f"w{n}_raw", [P, T, DI]) for n in "1g2"]
        w_hi = [sb(f"w{n}_hi", [P, T, DI], F32R) for n in "1g2"]
        w_lo = [sb(f"w{n}_lo", [P, T, DI], F32R) for n in "1g2"]
        logits = sb("logits", [P, T, NE])
        lmax = sb("lmax", [P, T])
        probs = sb("probs", [P, T, NE])
        psum_ = sb("psum_", [P, T])
        biased = sb("biased", [P, T, NE])
        gt = sb("gt", [P, T, NE, NE])
        eq = sb("eq", [P, T, NE, NE])
        pause = sb("pause", [P, 1])
        rank = sb("rank", [P, T, NE])
        coef = sb("coef", [P, T, NE])

        ps_h1 = [ctx.enter_context(nc.psum_tensor(f"ps_h1{i}", [P, L], F32)) for i in range(2)]
        ps_hg = [ctx.enter_context(nc.psum_tensor(f"ps_hg{i}", [P, L], F32)) for i in range(2)]
        ps_y = [ctx.enter_context(nc.psum_tensor(f"ps_y{i}", [P, L], F32)) for i in range(3)]
        ps_m = ctx.enter_context(nc.psum_tensor("ps_m", [P, L], F32))
        front_ps = [*ps_y, ps_m]
        mid_ps = [ps_h1[0], ps_hg[0], ps_h1[1], ps_hg[1]]

        const_ld = sem("const_ld")
        setup_v = sem("setup_v")
        setup_a = sem("setup_a")
        ctx_ld = sem("ctx_ld")
        xz_ld = sem("xz_ld")
        xres_ld = sem("xres_ld")
        bc_ld0 = sem("bc_ld0")
        bc_ld1 = sem("bc_ld1")
        xd_st = sem("xd_st")
        out_st = sem("out_st")
        raw_ld0 = sem("raw_ld0")
        raw_ld1 = sem("raw_ld1")
        raw_ld2 = sem("raw_ld2")
        inproj_done = sem("inproj_done")
        tap0_done = sem("tap0_done")
        conv_done = sem("conv_done")
        ut_done = sem("ut_done")
        u_ready = sem("u_ready")
        xp_done = sem("xp_done")
        xd_ready = sem("xd_ready")
        yinit_done = sem("yinit_done")
        dt_done = sem("dt_done")
        dt_read = sem("dt_read")
        e_ready = sem("e_ready")
        ln_ready = sem("ln_ready")
        sp_chain = sem("sp_chain")
        delta_ready = sem("delta_ready")
        du_ready = sem("du_ready")
        zstat = sem("zstat")
        zvar = sem("zvar")
        mv_done = sem("mv_done")
        zrstd = sem("zrstd")
        zn_ready = sem("zn_ready")
        zt_ready = sem("zt_ready")
        z_ready = sem("z_ready")
        zero_done = sem("zero_done")
        da_ready = sem("da_ready")
        bmul_done = sem("bmul_done")
        scan_done = sem("scan_done")
        cmul_done = sem("cmul_done")
        yadd_done = sem("yadd_done")
        y_ready = sem("y_ready")
        yt_done = sem("yt_done")
        x1_ready = sem("x1_ready")
        x2stat = sem("x2stat")
        x2var = sem("x2var")
        x2rstd = sem("x2rstd")
        x2_ready = sem("x2_ready")
        xt_done = sem("xt_done")
        xh_ready = sem("xh_ready")
        xl_ready = sem("xl_ready")
        gl_done = sem("gl_done")
        logit_read = sem("logit_read")
        r_chain = sem("r_chain")
        r_sub = sem("r_sub")
        r_exp = sem("r_exp")
        coef_ready = sem("coef_ready")
        h1_done = sem("h1_done")
        hg_done = sem("hg_done")
        t_done = sem("t_done")
        m_done = sem("m_done")
        h_made = sem("h_made")
        hh_ready = sem("hh_ready")
        hl_ready = sem("hl_ready")
        y_done = sem("y_done")
        acc_done = sem("acc_done")
        w1h = sem("w1h")
        wgh = sem("wgh")
        w2h = sem("w2h")
        w1l = sem("w1l")
        wgl = sem("wgl")
        w2l = sem("w2l")
        raw_ld = [raw_ld0, raw_ld1, raw_ld2]
        bc_ld = [bc_ld0, bc_ld1]
        NCONST = 15

        def some(count):
            return not (isinstance(count, int) and count <= 0)

        block = ctx.enter_context(nc.Block())

        @block.sync
        def _(sp):
            def bcast(a, n):
                return a.rearrange("(a n) -> a n", a=1).broadcast_to([P, n])

            small = [
                (in_w[:], t["in_wT"].rearrange("(k p) e -> p k e", p=P)),
                (conv_w[:], t["conv_w"].rearrange("(t p) c -> p t c", p=P)),
                (conv_b[:], t["conv_b"]),
                (xproj_w[:], t["xproj_wT"].rearrange("(t p) c -> p t c", p=P)),
                (dt_w[:], t["dt_wT"]),
                (dt_b[:], t["dt_b"]),
                (neg_A[:], t["A_log"].rearrange("(t p) c -> p t c", p=P)),
                (half_D[:], t["D"]),
                (gates[:, 0:1], bcast(t["g_xattn"], 1)),
                (gates[:, 1:2], bcast(t["g_ffn"], 1)),
                (gw_raw[:, :, 0:NE], t["gate_w"].rearrange("(t p) c -> p t c", p=P)),
                (gate_b[:], bcast(t["gate_b"], NE)),
                (biases[:], bcast(t["biases"], NE)),
                (ident[:], t["ident"]),
                (earlier[:].rearrange("p a b -> p (a b)"), bcast(t["earlier"], NE * NE)),
            ]

            def load_front(m):
                if some(T * m):
                    sp.wait_ge(inproj_done, T * m)
                sp.dma_start(ctxT[:], t["ctxT"][bass.ds(m, 1)].rearrange("a (k p) l -> p (a k) l", p=P)).then_inc(ctx_ld, 16)
                if some(DS * m):
                    sp.wait_ge(scan_done, DS * m)
                sp.dma_start(dA[1][:], t["x"][bass.ds(m, 1)].rearrange("a (i p) d -> p (a i) d", p=P)).then_inc(xz_ld, 16)

            def store_xd(m):
                sp.wait_ge(xd_ready, m + 1)
                sp.dma_start(xd_dram[bass.ds(m, 1)].rearrange("a r l -> (a r) l"), xdbl[DR:XP, :]).then_inc(xd_st, 16)

            def load_bc(m, n, odd):
                if isinstance(n, int) and n < 2:
                    sp.wait_ge(xd_st, 16 * (m + 1))
                else:
                    sp.wait_ge(cmul_done, DS * m + n - 1)
                src = xd_dram[bass.ds(m, 1)].rearrange("a (c n) l -> n a c l", c=2)[bass.ds(n, 1)]
                src = src.rearrange("n a c l -> (n a) c l").broadcast_to([P, 2, L])
                sp.dma_start(bc[odd][:], src).then_inc(bc_ld[odd], 16)

            def load_weights(step, e):
                for w, (routed, shared) in enumerate((("W1", "Ws1"), ("Wg", "Wsg"), ("W2", "Ws2"))):
                    hi, lo = ((w1h, w1l), (wgh, wgl), (w2h, w2l))[w]
                    if some(T * step):
                        sp.wait_ge(hi, T * step)
                    if some(T * step):
                        sp.wait_ge(lo, T * step)
                    src = t[shared] if e is None else t[routed][bass.ds(e, 1)].rearrange("a d h -> (a d) h")
                    sp.dma_start(w_raw[w][:], src.rearrange("(k p) h -> p k h", p=P)).then_inc(raw_ld[w], 16)

            def load_residual(m):
                if some(16 * m):
                    sp.wait_ge(out_st, 16 * m)
                sp.dma_start(acc[:], t["x"][bass.ds(m, 1)].rearrange("a (i p) d -> p (a i) d", p=P)).then_inc(xres_ld, 16)

            def store_out(b):
                sp.wait_ge(acc_done, T * STEPS * (b + 1))
                sp.dma_start(out[bass.ds(b, 1)].rearrange("a (i p) d -> p (a i) d", p=P), acc[:]).then_inc(out_st, 16)

            sp.dma_start(ctxT[:], t["ctxT"][0].rearrange("(k p) l -> p k l", p=P)).then_inc(ctx_ld, 16)
            for dst, src in small:
                sp.dma_start(dst, src).then_inc(const_ld, 16)
            sp.dma_start(dA[1][:], t["x"][0].rearrange("(i p) d -> p i d", p=P)).then_inc(xz_ld, 16)
            load_residual(0)
            store_xd(0)
            for n in range(2):
                load_bc(0, n, n)
            load_weights(0, None)
            with sp.Fori(1, DS // 2) as i:
                load_bc(0, 2 * i, 0)
                load_bc(0, 2 * i + 1, 1)
            load_weights(1, 0)
            with sp.Fori(0, NB - 1) as b:
                load_front(b + 1)
                store_xd(b + 1)
                load_bc(b + 1, 0, 0)
                load_bc(b + 1, 1, 1)
                with sp.Fori(0, NE - 1) as e:
                    load_weights(STEPS * b + e + 2, e + 1)
                    load_bc(b + 1, 2 * e + 2, 0)
                    load_bc(b + 1, 2 * e + 3, 1)
                load_weights(STEPS * b + STEPS, None)
                for n in range(2 * NE, DS):
                    load_bc(b + 1, n, n % 2)
                store_out(b)
                load_residual(b + 1)
                load_weights(STEPS * b + STEPS + 1, 0)
            with sp.Fori(0, NE - 1) as e:
                load_weights(STEPS * (NB - 1) + e + 2, e + 1)
            store_out(NB - 1)
            sp.wait_ge(out_st, 16 * NB)

        @block.tensor
        def _(pe):
            def three_passes(out_, lhs, rhs, sides, first, last):
                for q, (a, c) in enumerate(sides):
                    mm = pe.matmul(out_, lhs[a], rhs[c], start=first and q == 0, stop=last and q == len(sides) - 1)
                return mm

            def in_proj(m):
                pe.wait_ge(ctx_ld, 16 * (m + 1))
                for et in range(T):
                    for k in range(KM):
                        mm = pe.matmul(front_ps[et][:], in_w[:, k, et * P:(et + 1) * P], ctxT[:, k, :],
                                       start=k == 0, stop=k == KM - 1)
                    mm.then_inc(inproj_done, 1)

            def x_proj(m):
                for et in range(T):
                    pe.wait_ge(u_ready, T * m + et + 1)
                    mm = pe.matmul(ps_m[0:XP, :], xproj_w[:, et, :], u[:, et, :], start=et == 0, stop=et == T - 1)
                mm.then_inc(xp_done, 1)

            def dt_proj(m):
                pe.wait_ge(xd_ready, m + 1)
                for et in range(T):
                    pe.matmul(mid_ps[et][:], dt_w[:, et * P:(et + 1) * P], xdbl[0:DR, :],
                              start=True, stop=True).then_inc(dt_done, 1)

            def back(m):
                pe.wait_ge(y_ready, m + 1)
                for i in range(T):
                    for et in range(T):
                        mm = pe.transpose(mid_ps[i][:, et * P:(et + 1) * P], yacc[:, et, i * P:(i + 1) * P], ident[:])
                    mm.then_inc(yt_done, 1)
                for i in range(T):
                    pe.wait_ge(x2_ready, T * m + i + 1)
                    for k in range(T):
                        mm = pe.transpose(front_ps[i][:, k * P:(k + 1) * P], st[0][:, i, k * P:(k + 1) * P], ident[:])
                    mm.then_inc(xt_done, 1)
                pe.wait_ge(xl_ready, T * (m + 1))
                for i in range(T):
                    for k in range(T):
                        lhs = [v[:, k, i * P:(i + 1) * P] for v in (x_hi, x_lo)]
                        mm = three_passes(ps_h1[0][:, i * 8:i * 8 + 8], lhs, [gw_hi[:, k, :], gw_lo[:, k, :]],
                                          ((0, 0), (0, 1), (1, 0)), k == 0, k == T - 1)
                mm.then_inc(gl_done, 1)

            def hidden(step, j):
                for w, (ps, hi, lo, done, free) in enumerate(((ps_h1, w1h, w1l, h1_done, m_done),
                                                             (ps_hg, wgh, wgl, hg_done, h_made))):
                    pe.wait_ge(hi, T * step + j + 1)
                    pe.wait_ge(lo, T * step + j + 1)
                    if j >= 2:
                        pe.wait_ge(free, T * step + j - 1)
                    for k in range(T):
                        mm = three_passes(ps[j % 2][:], [v[w][:, k, j * P:(j + 1) * P] for v in (w_hi, w_lo)],
                                          [x_hi[:, k, :], x_lo[:, k, :]], ((0, 0), (0, 1), (1, 0)), k == 0, k == T - 1)
                    mm.then_inc(done, 1)

            def expert_out(step, tiles):
                for j in range(T):
                    pe.wait_ge(hh_ready, T * step + j + 1)
                    pe.wait_ge(w2h, T * step + j + 1)
                    pe.wait_ge(w2l, T * step + j + 1)
                    for i in tiles:
                        three_passes(ps_y[i % 3][:], [h_hi[:, j, i * P:(i + 1) * P]], [w_hi[2][:, j, :], w_lo[2][:, j, :]],
                                     ((0, 0), (0, 1)), j == 0, False)
                for i in tiles:
                    for j in range(T):
                        pe.wait_ge(hl_ready, T * step + j + 1)
                        mm = pe.matmul(ps_y[i % 3][:], h_lo[:, j, i * P:(i + 1) * P], w_hi[2][:, j, :],
                                       start=False, stop=j == T - 1)
                    mm.then_inc(y_done, 1)

            def step_(step, m=None):
                for j in range(T):
                    hidden(step, j)
                if m is not None:
                    x_proj(m)
                if m is not None:
                    pe.wait_ge(conv_done, T * (DC - 1) * (m + 1))
                else:
                    if some(T * step):
                        pe.wait_ge(acc_done, T * step)
                expert_out(step, (0, 1))
                if m is not None:
                    pe.wait_ge(h_made, T * (step + 1))
                    dt_proj(m)
                expert_out(step, (2,))
                pe.wait_ge(acc_done, T * step + 1)
                if m is not None:
                    pe.wait_ge(dt_read, T * (m + 1))
                expert_out(step, (3,))

            def first_step(b):
                pe.wait_ge(x1_ready, T * (b + 1))
                pe.wait_ge(logit_read, b + 1)

            pe.wait_ge(const_ld, 16 * NCONST)
            in_proj(0)
            pe.wait_ge(setup_v, 1)
            x_proj(0)
            dt_proj(0)
            pe.wait_ge(dt_read, T)
            back(0)
            with pe.Fori(0, NB - 1) as b:
                pe.wait_ge(xl_ready, T * (b + 1))
                in_proj(b + 1)
                first_step(b)
                step_(STEPS * b, b + 1)
                with pe.Fori(0, NE) as e:
                    step_(STEPS * b + e + 1)
                pe.wait_ge(acc_done, T * STEPS * (b + 1))
                back(b + 1)
            first_step(NB - 1)
            with pe.Fori(0, STEPS) as e:
                step_(STEPS * (NB - 1) + e)

        @block.scalar
        def _(act):
            def front_conv(m):
                if some(DS * m):
                    act.wait_ge(bmul_done, DS * m)
                for et in range(T):
                    act.wait_ge(inproj_done, T * m + et + 1)
                    act.activation(u[:, et, :], front_ps[et][:], ACT.Identity, bias=conv_b[:, et:et + 1],
                                   scale=conv_w[:, et, DC - 1:DC]).then_inc(tap0_done, 1)

            def front_tanh(m):
                if some(DS * m):
                    act.wait_ge(scan_done, DS * m)
                for et in range(T):
                    act.wait_ge(conv_done, T * (DC - 1) * m + T * (DC - 2) + et + 1)
                    act.activation(dA[0][:, et, :], u[:, et, :], ACT.Tanh, scale=0.5).then_inc(ut_done, 1)

            def front_z(m):
                act.wait_ge(zn_ready, T * (m + 1))
                if some(m):
                    act.wait_ge(yadd_done, T * DS * m)
                if some(T * m):
                    act.wait_ge(xt_done, T * m)
                act.activation(st[0][:], dA[1][:], ACT.Tanh, scale=0.5).then_inc(zt_ready, 1)

            def front_yinit(m):
                if some(T * m):
                    act.wait_ge(yt_done, T * m)
                for et in range(T):
                    act.wait_ge(u_ready, T * m + et + 1)
                    act.activation(yacc[:, et, :], u[:, et, :], ACT.Copy, scale=half_D[:, et:et + 1]).then_inc(yinit_done, 1)

            def front_xd(m):
                act.wait_ge(xp_done, m + 1)
                if some(16 * m):
                    act.wait_ge(xd_st, 16 * m)
                if some(T * m):
                    act.wait_ge(dt_done, T * m)
                act.activation(xdbl[:], ps_m[0:XP, :], ACT.Copy).then_inc(xd_ready, 1)

            def front_softplus(m):
                act.wait_ge(u_ready, T * (m + 1))
                if some(DS * m):
                    act.wait_ge(bmul_done, DS * m)
                for et in range(T):
                    act.wait_ge(dt_done, T * m + et + 1)
                    act.activation(dA[0][:, et, :], mid_ps[et][:], ACT.Abs, bias=dt_b[:, et:et + 1])
                    act.activation(delta[:, et, :], mid_ps[et][:], ACT.Relu, bias=dt_b[:, et:et + 1]).then_inc(dt_read, 1)
                act.wait_ge(dt_read, T * (m + 1))
                act.activation(dA[0][:], dA[0][:], ACT.Exp, scale=-1.0).then_inc(e_ready, 1)
                act.wait_ge(z_ready, m + 1)
                act.wait_ge(e_ready, m + 1)
                act.activation(st[0][:], dA[0][:], ACT.Ln, bias=ones[:, 0:1]).then_inc(ln_ready, 1)

            def decay(N, n, odd, tiles):
                if some(N - 1):
                    act.wait_ge(scan_done, N - 1)
                for et in tiles:
                    a = act.activation(dA[odd][:, et, 1:L], delta[:, et, 1:L], ACT.Exp, scale=neg_A[:, et, bass.ds(n, 1)])
                    a.then_inc(da_ready, 1)

            def back(m):
                for i in range(T):
                    act.wait_ge(xt_done, T * m + i + 1)
                    ps = front_ps[i][:].rearrange("p (k l) -> p k l", k=T)
                    act.activation(x_hi[:, :, i * P:(i + 1) * P], ps, ACT.Copy).then_inc(xh_ready, 1)
                act.wait_ge(r_sub, m + 1)
                act.activation(probs[:], logits[:], ACT.Exp).then_inc(r_exp, 1)

            def split_hi(step, w, name, j):
                act.wait_ge(raw_ld[w], 16 * (step + 1))
                sel = (slice(None), slice(None), slice(j * P, (j + 1) * P)) if w < 2 else (slice(None), j)
                act.activation(w_hi[w][sel], w_raw[w][sel], ACT.Copy).then_inc(name, 1)

            def step_(step, between, after=None, split=True):
                for j in range(T):
                    act.wait_ge(h1_done, T * step + j + 1)
                    if j >= 2:
                        act.wait_ge(hl_ready, T * step + j - 1)
                    act.activation(h_tmp[j % 2][:], ps_h1[j % 2][:], ACT.Tanh, scale=0.5).then_inc(t_done, 1)
                    between(j)
                    act.wait_ge(h_made, T * step + j + 1)
                    act.activation(h_hi[:, j, :], h_tmp[j % 2][:], ACT.Copy).then_inc(hh_ready, 1)
                    if split:
                        act.wait_ge(hg_done, T * step + j + 1)
                        split_hi(step + 1, 0, w1h, j)
                        split_hi(step + 1, 1, wgh, j)
                if after:
                    after()
                if split:
                    act.wait_ge(y_done, T * (step + 1))
                    for j in range(T):
                        split_hi(step + 1, 2, w2h, j)

            def nothing(j):
                pass

            def two_states(m, n):
                def between(j):
                    decay(DS * m + n + j // 2, n + j // 2, j // 2, (2 * (j % 2), 2 * (j % 2) + 1))
                return between

            def four_states(m, n):
                def between(j):
                    decay(DS * m + n + j, n + j, j % 2, range(T))
                return between

            act.wait_ge(const_ld, 16 * NCONST)
            act.activation(gate_tanh[:], gates[:], ACT.Tanh).then_inc(setup_a, 1)
            act.activation(neg_A[:], neg_A[:], ACT.Exp).then_inc(setup_a, 1)
            act.wait_ge(setup_v, 1)
            front_conv(0)
            front_tanh(0)
            front_yinit(0)
            front_z(0)
            front_xd(0)
            front_softplus(0)
            act.wait_ge(delta_ready, 1)
            act.wait_ge(zero_done, 1)
            decay(0, 0, 0, range(T))
            decay(1, 1, 1, range(T))
            with act.Fori(1, DS // 2) as i:
                decay(2 * i, 2 * i, 0, range(T))
                decay(2 * i + 1, 2 * i + 1, 1, range(T))
            for j in range(T):
                split_hi(0, 0, w1h, j)
                split_hi(0, 1, wgh, j)
            for j in range(T):
                split_hi(0, 2, w2h, j)
            back(0)
            with act.Fori(0, NB - 1) as b:
                front_conv(b + 1)

                def front(j):
                    if j == 0:
                        front_tanh(b + 1)
                    if j == 2:
                        front_yinit(b + 1)
                        front_z(b + 1)

                def front_end():
                    front_xd(b + 1)
                    front_softplus(b + 1)

                step_(STEPS * b, front, front_end)
                act.wait_ge(delta_ready, b + 2)
                act.wait_ge(zero_done, b + 2)
                with act.Fori(0, NE - 1) as e:
                    step_(STEPS * b + e + 1, two_states(b + 1, 2 * e))
                step_(STEPS * b + NE, four_states(b + 1, 2 * (NE - 1)))
                back(b + 1)
            with act.Fori(0, STEPS - 1) as e:
                step_(STEPS * (NB - 1) + e, nothing)
            step_(STEPS * NB - 1, nothing, split=False)

        @block.vector
        def _(dve):
            def front_conv(m):
                for k in range(DC - 1):
                    back_ = DC - 1 - k
                    for et in range(T):
                        if k == 0:
                            dve.wait_ge(tap0_done, T * m + et + 1)
                        else:
                            dve.wait_ge(conv_done, T * (DC - 1) * m + T * (k - 1) + et + 1)
                        dve.scalar_tensor_tensor(out=u[:, et, back_:L], in0=front_ps[et][:, 0:L - back_],
                                                 scalar=conv_w[:, et, k:k + 1], in1=u[:, et, back_:L],
                                                 op0=ALU.mult, op1=ALU.add).then_inc(conv_done, 1)

            def front_silu(m):
                for et in range(T):
                    dve.wait_ge(ut_done, T * m + et + 1)
                    dve.scalar_tensor_tensor(out=u[:, et, :], in0=dA[0][:, et, :], scalar=1.0, in1=u[:, et, :],
                                             op0=ALU.add, op1=ALU.mult).then_inc(u_ready, 1)

            def mean_and_var(m, stat_done, var_done):
                dve.wait_ge(stat_done, T * (m + 1))
                dve.memset(pause[:], 0.0)
                for i in range(T):
                    last = dve.bn_aggr(mv[:, i, :], bn[:, i, :])
                last.then_inc(mv_done, 1)
                dve.wait_ge(mv_done, 2 * m + (1 if stat_done is zstat else 2))
                dve.tensor_scalar(var_eps[:], mv[:, :, 1], EPS, None, ALU.add).then_inc(var_done, 1)

            def front_z(m):
                dve.wait_ge(xz_ld, 16 * (m + 1))
                for i in range(T):
                    dve.bn_stats(bn[:, i, :], dA[1][:, i, :]).then_inc(zstat, 1)
                mean_and_var(m, zstat, zvar)
                dve.wait_ge(zrstd, m + 1)
                for i in range(T):
                    dve.tensor_scalar(dA[1][:, i, :], dA[1][:, i, :], mv[:, i, 0:1], rstd[:, i:i + 1],
                                      ALU.subtract, ALU.mult).then_inc(zn_ready, 1)

            def front_z2(m):
                dve.wait_ge(zt_ready, m + 1)
                dve.scalar_tensor_tensor(out=z2[:], in0=st[0][:], scalar=1.0, in1=dA[1][:],
                                         op0=ALU.add, op1=ALU.mult).then_inc(z_ready, 1)

            def front_delta(m):
                dve.wait_ge(e_ready, m + 1)
                dve.tensor_scalar(st[1][:], dA[0][:], 1.0, None, ALU.add).then_inc(sp_chain, 1)
                dve.wait_ge(sp_chain, 3 * m + 1)
                dve.scalar_tensor_tensor(out=st[1][:], in0=st[1][:], scalar=-1.0, in1=dA[0][:],
                                         op0=ALU.add, op1=ALU.subtract).then_inc(sp_chain, 1)
                dve.wait_ge(ln_ready, m + 1)
                dve.wait_ge(sp_chain, 3 * m + 2)
                dve.tensor_tensor(st[0][:], st[0][:], st[1][:], ALU.subtract).then_inc(sp_chain, 1)
                dve.wait_ge(sp_chain, 3 * m + 3)
                dve.tensor_tensor(delta[:], delta[:], st[0][:], ALU.add).then_inc(delta_ready, 1)
                dve.wait_ge(delta_ready, m + 1)
                dve.wait_ge(yinit_done, T * (m + 1))
                dve.wait_ge(xp_done, m + 1)
                dve.scalar_tensor_tensor(out=u[:], in0=delta[:], scalar=0.5, in1=u[:],
                                         op0=ALU.mult, op1=ALU.mult).then_inc(du_ready, 1)
                dve.wait_ge(z_ready, m + 1)
                dve.memset(dA[0][:, :, 0:1], 0.0)
                dve.memset(dA[1][:, :, 0:1], 0.0).then_inc(zero_done, 1)

            def bmul(m, N, odd, turn):
                dve.wait_ge(bc_ld[odd], 16 * turn)
                dve.wait_ge(du_ready, m + 1)
                if some(T * (N - 1)):
                    dve.wait_ge(yadd_done, T * (N - 1))
                dve.tensor_tensor(st[odd][:], u[:], bc[odd][:, 0:1, :].broadcast_to([P, T, L]),
                                  ALU.mult).then_inc(bmul_done, 1)

            def scan(N, odd):
                dve.wait_ge(bmul_done, N + 1)
                dve.wait_ge(da_ready, T * (N + 1))
                flat = [v[odd][:].rearrange("p t l -> p (t l)") for v in (dA, st)]
                dve.tensor_tensor_scan(flat[1], flat[0], flat[1], 0.0, ALU.mult, ALU.add).then_inc(scan_done, 1)

            def cmul(N, odd):
                dve.wait_ge(scan_done, N + 1)
                dve.tensor_tensor(st[odd][:], st[odd][:], bc[odd][:, 1:2, :].broadcast_to([P, T, L]),
                                  ALU.mult).then_inc(cmul_done, 1)

            def back(m):
                dve.wait_ge(yadd_done, T * DS * (m + 1))
                dve.scalar_tensor_tensor(out=yacc[:], in0=yacc[:], scalar=0.5, in1=z2[:],
                                         op0=ALU.mult, op1=ALU.mult).then_inc(y_ready, 1)
                dve.wait_ge(xres_ld, 16 * (m + 1))
                for i in range(T):
                    dve.wait_ge(yt_done, T * m + i + 1)
                    dve.scalar_tensor_tensor(out=acc[:, i, :], in0=mid_ps[i][:], scalar=gate_tanh[:, 0:1],
                                             in1=acc[:, i, :], op0=ALU.mult, op1=ALU.add).then_inc(x1_ready, 1)
                    dve.wait_ge(x1_ready, T * m + i + 1)
                    dve.bn_stats(bn[:, i, :], acc[:, i, :]).then_inc(x2stat, 1)
                mean_and_var(m, x2stat, x2var)
                dve.wait_ge(x2rstd, m + 1)
                for i in range(T):
                    dve.tensor_scalar(st[0][:, i, :], acc[:, i, :], mv[:, i, 0:1], rstd[:, i:i + 1],
                                      ALU.subtract, ALU.mult).then_inc(x2_ready, 1)
                for i in range(T):
                    dve.wait_ge(xh_ready, T * m + i + 1)
                    cols = slice(i * P, (i + 1) * P)
                    dve.tensor_tensor(x_lo[:, :, cols], front_ps[i][:].rearrange("p (k l) -> p k l", k=T),
                                      x_hi[:, :, cols].bitcast(F32), ALU.subtract).then_inc(xl_ready, 1)
                router(m)

            def router(m):
                links = 11
                done = [0]

                def link(ins):
                    done[0] += 1
                    ins.then_inc(r_chain, 1)
                    dve.wait_ge(r_chain, links * m + done[0])

                def over(v):
                    return v.rearrange("p (t a) -> p t a", a=1).broadcast_to([P, T, NE])

                dve.wait_ge(gl_done, m + 1)
                ps = ps_h1[0][:, 0:8 * T].rearrange("p (i e) -> p i e", e=8)[:, :, 0:NE]
                gb = gate_b[:].rearrange("p (a e) -> p a e", a=1).broadcast_to([P, T, NE])
                bb = biases[:].rearrange("p (a e) -> p a e", a=1).broadcast_to([P, T, NE])
                dve.tensor_tensor(logits[:], ps, gb, ALU.add).then_inc(logit_read, 1)
                dve.wait_ge(logit_read, m + 1)
                link(dve.tensor_reduce(lmax[:], logits[:], AX_X, ALU.max))
                dve.tensor_tensor(logits[:], logits[:], over(lmax[:]), ALU.subtract).then_inc(r_sub, 1)
                dve.wait_ge(r_exp, m + 1)
                link(dve.tensor_reduce(psum_[:], probs[:], AX_X, ALU.add))
                link(dve.reciprocal(psum_[:], psum_[:]))
                link(dve.tensor_tensor(probs[:], probs[:], over(psum_[:]), ALU.mult))
                link(dve.tensor_tensor(biased[:], probs[:], bb, ALU.add))
                mine = biased[:].rearrange("p t (e a) -> p t e a", a=1).broadcast_to([P, T, NE, NE])
                other = biased[:].rearrange("p t (a e) -> p t a e", a=1).broadcast_to([P, T, NE, NE])
                tie = earlier[:].rearrange("p (a e) f -> p a e f", a=1).broadcast_to([P, T, NE, NE])
                for i in range(T):
                    dve.tensor_tensor(eq[:, i], other[:, i], mine[:, i], ALU.is_equal)
                    last = dve.tensor_tensor(gt[:, i], other[:, i], mine[:, i], ALU.is_gt)
                link(last)
                for i in range(T):
                    last = dve.tensor_tensor(eq[:, i], eq[:, i], tie[:, i], ALU.mult)
                link(last)
                link(dve.tensor_tensor(gt[:], gt[:], eq[:], ALU.add))
                link(dve.tensor_reduce(rank[:], gt[:], AX_X, ALU.add))
                link(dve.scalar_tensor_tensor(out=coef[:], in0=rank[:], scalar=float(TOP_K), in1=probs[:],
                                              op0=ALU.is_lt, op1=ALU.mult))
                link(dve.tensor_reduce(psum_[:], coef[:], AX_X, ALU.add))
                dve.reciprocal(psum_[:], psum_[:]).then_inc(coef_ready, 1)
                dve.wait_ge(coef_ready, 2 * m + 1)
                dve.scalar_tensor_tensor(out=coef[:], in0=coef[:], scalar=half_tgf[:, 0:1], in1=over(psum_[:]),
                                         op0=ALU.mult, op1=ALU.mult).then_inc(coef_ready, 1)
                dve.wait_ge(coef_ready, 2 * m + 2)
                assert done[0] == links

            def split_lo(step, j):
                dve.wait_ge(w1h, T * step + j + 1)
                cols = slice(j * P, (j + 1) * P)
                dve.tensor_tensor(w_lo[0][:, :, cols], w_raw[0][:, :, cols], w_hi[0][:, :, cols].bitcast(F32),
                                  ALU.subtract).then_inc(w1l, 1)

            def step_(step, e, between, split=True):
                def add_out(i):
                    dve.wait_ge(y_done, T * step + i + 1)
                    if e is not None or i > 0:
                        dve.wait_ge(acc_done, T * step + i)
                    scale = half_tgf[:, 0:1] if e is None else coef[:, i, bass.ds(e, 1)]
                    dve.scalar_tensor_tensor(out=acc[:, i, :], in0=ps_y[i % 3][:], scalar=scale, in1=acc[:, i, :],
                                             op0=ALU.mult, op1=ALU.add).then_inc(acc_done, 1)

                for j in range(T):
                    dve.wait_ge(t_done, T * step + j + 1)
                    dve.scalar_tensor_tensor(out=h_tmp[j % 2][:], in0=h_tmp[j % 2][:], scalar=1.0, in1=ps_h1[j % 2][:],
                                             op0=ALU.add, op1=ALU.mult).then_inc(m_done, 1)
                    dve.wait_ge(m_done, T * step + j + 1)
                    dve.wait_ge(hg_done, T * step + j + 1)
                    dve.tensor_tensor(h_tmp[j % 2][:], h_tmp[j % 2][:], ps_hg[j % 2][:], ALU.mult).then_inc(h_made, 1)
                    if split:
                        split_lo(step + 1, j)
                    between(j)
                add_out(0)
                add_out(1)
                between(T)
                add_out(2)
                add_out(3)
                between(T + 1)

            def nothing(k):
                pass

            def states(m, n, turn, count):
                def between(k):
                    for q in range(k * count // 2, (k + 1) * count // 2):
                        N, odd = DS * m + n + q // 3, (q // 3) % 2
                        if q % 3 == 0:
                            bmul(m, N, odd, turn + q // 6)
                        elif q % 3 == 1:
                            scan(N, odd)
                        else:
                            cmul(N, odd)
                return between

            dve.memset(ones[:], 1.0)
            dve.memset(gw_raw[:, :, NE:NE + 1], 0.0).then_inc(setup_v, 1)
            dve.memset(minus_half[:], -0.5).then_inc(setup_v, 1)
            dve.wait_ge(setup_v, 2)
            dve.wait_ge(const_ld, 16 * NCONST)
            dve.tensor_scalar(xproj_w[:], xproj_w[:], 0.5, None, ALU.mult).then_inc(setup_v, 1)
            dve.tensor_scalar(half_D[:], half_D[:], 0.5, None, ALU.mult).then_inc(setup_v, 1)
            dve.tensor_copy(gw_hi[:], gw_raw[:]).then_inc(setup_v, 1)
            dve.wait_ge(setup_v, 5)
            dve.tensor_tensor(gw_lo[:], gw_raw[:], gw_hi[:].bitcast(F32), ALU.subtract).then_inc(setup_v, 1)
            dve.wait_ge(setup_a, 2)
            dve.tensor_scalar(half_tgf[:], gate_tanh[:, 1:2], 0.5, None, ALU.mult).then_inc(setup_v, 1)
            dve.tensor_scalar(neg_A[:], neg_A[:], -1.0, None, ALU.mult).then_inc(setup_v, 1)
            dve.wait_ge(setup_v, 8)
            front_conv(0)
            front_silu(0)
            front_z(0)
            front_z2(0)
            front_delta(0)
            for n in range(2):
                bmul(0, n, n, 1)
                scan(n, n)
                cmul(n, n)
            with dve.Fori(1, DS // 2) as i:
                for odd in range(2):
                    bmul(0, 2 * i + odd, odd, i + 1)
                    scan(2 * i + odd, odd)
                    cmul(2 * i + odd, odd)
            for j in range(T):
                split_lo(0, j)
            back(0)
            with dve.Fori(0, NB - 1) as b:
                front_conv(b + 1)

                def front(k):
                    if k == 0:
                        front_silu(b + 1)
                    if k == 1:
                        front_z(b + 1)
                    if k == 2:
                        front_z2(b + 1)
                    if k == T + 1:
                        front_delta(b + 1)

                step_(STEPS * b, None, front)
                with dve.Fori(0, NE - 1) as e:
                    step_(STEPS * b + e + 1, e, states(b + 1, 2 * e, DS // 2 * (b + 1) + e + 1, 2))
                step_(STEPS * b + NE, NE - 1, states(b + 1, 2 * (NE - 1), DS // 2 * (b + 1) + NE, 4))
                back(b + 1)
            step_(STEPS * (NB - 1), None, nothing)
            with dve.Fori(0, NE - 1) as e:
                step_(STEPS * (NB - 1) + e + 1, e, nothing)
            step_(STEPS * NB - 1, NE - 1, nothing, split=False)

        @block.gpsimd
        def _(pool):
            def power(sem_var, sem_rstd, m):
                pool.wait_ge(sem_var, m + 1)
                pool.tensor_tensor(rstd[:], var_eps[:], minus_half[:], ALU.pow).then_inc(sem_rstd, 1)

            def y_add(m, N, odd):
                pool.wait_ge(yinit_done, T * (m + 1))
                pool.wait_ge(cmul_done, N + 1)
                for et in range(T):
                    if some(T * N + et - T + 1):
                        pool.wait_ge(yadd_done, T * N + et - T + 1)
                    pool.tensor_tensor(yacc[:, et, :], yacc[:, et, :], st[odd][:, et, :], ALU.add).then_inc(yadd_done, 1)

            def split_lo(step, w, hi, lo, j):
                pool.wait_ge(hi, T * step + j + 1)
                sel = (slice(None), slice(None), slice(j * P, (j + 1) * P)) if w < 2 else (slice(None), j)
                pool.tensor_tensor(w_lo[w][sel], w_raw[w][sel], w_hi[w][sel].bitcast(F32), ALU.subtract).then_inc(lo, 1)

            def step_(step, m=None, N=None, states=0, front=None, split=True):
                for j in range(T):
                    pool.wait_ge(hh_ready, T * step + j + 1)
                    pool.tensor_tensor(h_lo[:, j, :], h_tmp[j % 2][:], h_hi[:, j, :].bitcast(F32),
                                       ALU.subtract).then_inc(hl_ready, 1)
                    if split:
                        split_lo(step + 1, 1, wgh, wgl, j)
                    if front and j == 0:
                        front()
                    if states == 4 and j == 2:
                        y_add(m, N, 0)
                if states:
                    y_add(m, N + states // 2 - 1, (states // 2 - 1) % 2)
                if split:
                    for j in range(T):
                        split_lo(step + 1, 2, w2h, w2l, j)
                for q in range(states // 2, states):
                    y_add(m, N + q, q % 2)

            pool.wait_ge(setup_v, 2)
            power(zvar, zrstd, 0)
            y_add(0, 0, 0)
            y_add(0, 1, 1)
            with pool.Fori(1, DS // 2) as i:
                y_add(0, 2 * i, 0)
                y_add(0, 2 * i + 1, 1)
            for j in range(T):
                split_lo(0, 1, wgh, wgl, j)
            for j in range(T):
                split_lo(0, 2, w2h, w2l, j)
            power(x2var, x2rstd, 0)
            with pool.Fori(0, NB - 1) as b:
                def front():
                    power(zvar, zrstd, b + 1)

                step_(STEPS * b, front=front)
                with pool.Fori(0, NE - 1) as e:
                    step_(STEPS * b + e + 1, m=b + 1, N=DS * (b + 1) + 2 * e, states=2)
                step_(STEPS * b + NE, m=b + 1, N=DS * (b + 1) + 2 * (NE - 1), states=4)
                power(x2var, x2rstd, b + 1)
            with pool.Fori(0, STEPS - 1) as e:
                step_(STEPS * (NB - 1) + e)
            step_(STEPS * NB - 1, split=False)


def kernel(**inputs):
    import numpy as np
    import concourse.bacc as bacc
    from concourse.bass_utils import run_bass_kernel_spmd

    g = {k.replace("L0_xattn_", "").replace("L0_ffn_", ""): np.asarray(v) for k, v in inputs.items()}
    ne = g["W1"].shape[0]

    def columns(v):
        return v.reshape(-1, P).T

    arrays = {
        "x": g["x"], "ctxT": g["ctx_1024"].transpose(0, 2, 1), "g_xattn": g["g_xattn"], "g_ffn": g["g_ffn"],
        "in_wT": g["in_proj_w"].T, "conv_w": g["conv_w"], "conv_b": columns(g["conv_b"]), "xproj_wT": g["x_proj_w"].T,
        "dt_wT": g["dt_proj_w"].T, "dt_b": columns(g["dt_proj_b"]), "A_log": g["A_log"], "D": columns(g["D"]),
        "W1": g["W1"], "Wg": g["Wg"], "W2": g["W2"], "Ws1": g["Ws1"], "Wsg": g["Wsg"], "Ws2": g["Ws2"],
        "gate_w": g["gate_w"], "gate_b": g["gate_b"], "biases": g["biases"],
        "ident": np.eye(P, dtype=np.float32), "earlier": np.tril(np.ones((ne, ne), np.float32), -1).reshape(-1),
    }
    nc = bacc.Bacc("TRN2", target_bir_lowering=False, num_devices=1)
    fed, args = {}, {}
    for name in NAMES:
        a = np.ascontiguousarray(arrays[name])
        fed[f"in_{name}_dram"] = a
        args[name] = nc.dram_tensor(f"in_{name}_dram", a.shape, mybir.dt.from_np(a.dtype), kind="ExternalInput").ap()
    out = nc.dram_tensor("out_dram", g["x"].shape, F32, kind="ExternalOutput").ap()
    gated_block(nc, args, out)
    return run_bass_kernel_spmd(nc, [fed], core_ids=[0]).results[0]["out_dram"]
```

```python
from contextlib import ExitStack

import concourse.bass as bass
from concourse import mybir

F32 = mybir.dt.float32
F32R = mybir.dt.float32r
ALU = mybir.AluOpType
ACT = mybir.ActivationFunctionType
AX_X = mybir.AxisListType.X

P = 128
NAMES = ["x", "ctxT", "g_xattn", "g_ffn", "in_wT", "conv_w", "conv_b", "xproj_wT", "dt_wT", "dt_b", "A_log", "D",
         "W1", "Wg", "W2", "Ws1", "Wsg", "Ws2", "gate_w", "gate_b", "biases", "ident", "earlier"]


def gated_block(nc, t, out):
    NB, L, DI = t["x"].shape
    DM = t["ctxT"].shape[1]
    NE = t["W1"].shape[0]
    DS = t["A_log"].shape[1]
    DC = t["conv_w"].shape[1]
    DR = t["dt_wT"].shape[0]
    XP = DR + 2 * DS
    TOP_K = 3
    EPS = 1e-5
    T = DI // P
    KM = DM // P
    STEPS = NE + 1
    assert L == DI and t["W1"].shape[1:] == (DI, DI)

    xd_dram = nc.dram_tensor("xd_scratch", (NB, 2 * DS, L), F32, kind="Internal").ap()

    with ExitStack() as ctx:
        def sb(name, shape, dt=F32):
            return ctx.enter_context(nc.sbuf_tensor(name, shape, dt))

        def sem(name):
            return ctx.enter_context(nc.semaphore(name))

        in_w = sb("in_w", [P, KM, DI])
        xproj_w = sb("xproj_w", [P, T, XP])
        dt_w = sb("dt_w", [DR, DI])
        conv_w = sb("conv_w", [P, T, DC])
        conv_b = sb("conv_b", [P, T])
        dt_b = sb("dt_b", [P, T])
        neg_A = sb("neg_A", [P, T, DS])
        half_D = sb("half_D", [P, T])
        gates = sb("gates", [P, 2])
        gate_tanh = sb("gate_tanh", [P, 2])
        half_tgf = sb("half_tgf", [P, 1])
        ones = sb("ones", [P, 1])
        minus_half = sb("minus_half", [P, T])
        gw_raw = sb("gw_raw", [P, T, NE])
        gw_hi = sb("gw_hi", [P, T, P], F32R)
        gw_lo = sb("gw_lo", [P, T, P], F32R)
        gate_b = sb("gate_b", [P, NE])
        biases = sb("biases", [P, NE])
        ident = sb("ident", [P, P])
        earlier = sb("earlier", [P, NE, NE])

        ctxT = sb("ctxT", [P, KM, L])
        u = sb("u", [P, T, L])
        delta = sb("delta", [P, T, L])
        yacc = sb("yacc", [P, T, L])
        z2 = sb("z2", [P, T, L])
        x1 = z2
        x_rows = delta
        xdbl = sb("xdbl", [XP, L])
        logits_T = xdbl[0:NE]
        bc = [sb(f"bc{i}", [P, 2, L]) for i in range(2)]
        dA = [sb(f"dA{i}", [P, T, L]) for i in range(2)]
        st = [sb(f"st{i}", [P, T, L]) for i in range(2)]
        gt, eq = (st[1][:, i, 0:T * NE * NE].rearrange("p (t a e) -> p t a e", t=T, a=NE) for i in range(2))
        bn = sb("bn", [P, T, 6])
        mv = sb("mv", [P, T, 2])
        var_eps = sb("var_eps", [P, T])
        rstd = sb("rstd", [P, T])

        acc = sb("acc", [P, T, DI])
        x_hi = sb("x_hi", [P, T, L], F32R)
        x_lo = sb("x_lo", [P, T, L], F32R)
        h_tmp = [sb(f"h_tmp{i}", [P, L]) for i in range(2)]
        h_hi = sb("h_hi", [P, T, L], F32R)
        h_lo = sb("h_lo", [P, T, L], F32R)
        w_raw = [sb(f"w{n}_raw", [P, T, DI]) for n in "1g2"]
        w_hi = [sb(f"w{n}_hi", [P, T, DI], F32R) for n in "1g2"]
        w_lo = [sb(f"w{n}_lo", [P, T, DI], F32R) for n in "1g2"]
        logits = sb("logits", [P, T, NE])
        lmax = sb("lmax", [P, T])
        probs = sb("probs", [P, T, NE])
        psum_ = sb("psum_", [P, T])
        biased = sb("biased", [P, T, NE])
        pause = sb("pause", [P, 1])
        rank = sb("rank", [P, T, NE])
        coef = sb("coef", [P, T, NE])

        ps_h1 = [ctx.enter_context(nc.psum_tensor(f"ps_h1{i}", [P, L], F32)) for i in range(2)]
        ps_hg = [ctx.enter_context(nc.psum_tensor(f"ps_hg{i}", [P, L], F32)) for i in range(2)]
        ps_y = [ctx.enter_context(nc.psum_tensor(f"ps_y{i}", [P, L], F32)) for i in range(3)]
        ps_m = ctx.enter_context(nc.psum_tensor("ps_m", [P, L], F32))
        front_ps = [*ps_y, ps_m]
        mid_ps = [ps_h1[0], ps_hg[0], ps_h1[1], ps_hg[1]]

        const_ld = sem("const_ld")
        setup_v = sem("setup_v")
        setup_a = sem("setup_a")
        ctx_ld = sem("ctx_ld")
        xz_ld = sem("xz_ld")
        xres_ld = sem("xres_ld")
        bc_ld0 = sem("bc_ld0")
        bc_ld1 = sem("bc_ld1")
        xd_st = sem("xd_st")
        out_st = sem("out_st")
        raw_ld0 = sem("raw_ld0")
        raw_ld1 = sem("raw_ld1")
        raw_ld2 = sem("raw_ld2")
        inproj_done = sem("inproj_done")
        tap0_done = sem("tap0_done")
        conv_done = sem("conv_done")
        ut_done = sem("ut_done")
        u_ready = sem("u_ready")
        xp_done = sem("xp_done")
        xd_ready = sem("xd_ready")
        yinit_done = sem("yinit_done")
        dt_done = sem("dt_done")
        dt_read = sem("dt_read")
        e_ready = sem("e_ready")
        ln_ready = sem("ln_ready")
        sp_chain = sem("sp_chain")
        delta_ready = sem("delta_ready")
        du_ready = sem("du_ready")
        zstat = sem("zstat")
        zvar = sem("zvar")
        mv_done = sem("mv_done")
        zrstd = sem("zrstd")
        zn_ready = sem("zn_ready")
        zt_ready = sem("zt_ready")
        z_ready = sem("z_ready")
        zero_done = sem("zero_done")
        da_ready = sem("da_ready")
        bmul_done = sem("bmul_done")
        scan_done = sem("scan_done")
        cmul_done = sem("cmul_done")
        yadd_done = sem("yadd_done")
        y_ready = sem("y_ready")
        yt_done = sem("yt_done")
        x1_ready = sem("x1_ready")
        x2stat = sem("x2stat")
        x2var = sem("x2var")
        x2rstd = sem("x2rstd")
        x2_ready = sem("x2_ready")
        xt_done = sem("xt_done")
        xh_ready = sem("xh_ready")
        xl_ready = sem("xl_ready")
        lt_done = sem("lt_done")
        lt_ready = sem("lt_ready")
        gl_done = sem("gl_done")
        logit_read = sem("logit_read")
        r_chain = sem("r_chain")
        r_sub = sem("r_sub")
        r_exp = sem("r_exp")
        coef_ready = sem("coef_ready")
        h1_done = sem("h1_done")
        hg_done = sem("hg_done")
        t_done = sem("t_done")
        m_done = sem("m_done")
        h_made = sem("h_made")
        hh_ready = sem("hh_ready")
        hl_ready = sem("hl_ready")
        y_done = sem("y_done")
        acc_done = sem("acc_done")
        w1h = sem("w1h")
        wgh = sem("wgh")
        w2h = sem("w2h")
        w1l = sem("w1l")
        wgl = sem("wgl")
        w2l = sem("w2l")
        raw_ld = [raw_ld0, raw_ld1, raw_ld2]
        bc_ld = [bc_ld0, bc_ld1]
        NCONST = 15

        def some(count):
            return not (isinstance(count, int) and count <= 0)

        block = ctx.enter_context(nc.Block())

        @block.sync
        def _(sp):
            def bcast(a, n):
                return a.rearrange("(a n) -> a n", a=1).broadcast_to([P, n])

            small = [
                (in_w[:], t["in_wT"].rearrange("(k p) e -> p k e", p=P)),
                (conv_w[:], t["conv_w"].rearrange("(t p) c -> p t c", p=P)),
                (conv_b[:], t["conv_b"]),
                (xproj_w[:], t["xproj_wT"].rearrange("(t p) c -> p t c", p=P)),
                (dt_w[:], t["dt_wT"]),
                (dt_b[:], t["dt_b"]),
                (neg_A[:], t["A_log"].rearrange("(t p) c -> p t c", p=P)),
                (half_D[:], t["D"]),
                (gates[:, 0:1], bcast(t["g_xattn"], 1)),
                (gates[:, 1:2], bcast(t["g_ffn"], 1)),
                (gw_raw[:, :, 0:NE], t["gate_w"].rearrange("(t p) c -> p t c", p=P)),
                (gate_b[:], bcast(t["gate_b"], NE)),
                (biases[:], bcast(t["biases"], NE)),
                (ident[:], t["ident"]),
                (earlier[:].rearrange("p a b -> p (a b)"), bcast(t["earlier"], NE * NE)),
            ]

            def load_ctx(m):
                if some(m):
                    sp.wait_ge(inproj_done, T * m)
                sp.dma_start(ctxT[:], t["ctxT"][bass.ds(m, 1)].rearrange("a (k p) l -> p (a k) l", p=P)).then_inc(ctx_ld, 16)

            def load_x(m):
                if some(m):
                    sp.wait_ge(scan_done, DS * m)
                sp.dma_start(dA[1][:], t["x"][bass.ds(m, 1)].rearrange("a (i p) d -> p (a i) d", p=P)).then_inc(xz_ld, 16)

            def load_x_rows(m):
                sp.wait_ge(da_ready, T * DS * (m + 1))
                sp.dma_start(x_rows[:], t["x"][bass.ds(m, 1)].rearrange("a (i p) d -> p (a i) d", p=P)).then_inc(xres_ld, 16)

            def store_xd(m):
                sp.wait_ge(xd_ready, m + 1)
                sp.dma_start(xd_dram[bass.ds(m, 1)].rearrange("a r l -> (a r) l"), xdbl[DR:XP, :]).then_inc(xd_st, 16)

            def load_bc(m, n, odd):
                if isinstance(n, int) and n < 2:
                    sp.wait_ge(xd_st, 16 * (m + 1))
                else:
                    sp.wait_ge(cmul_done, DS * m + n - 1)
                src = xd_dram[bass.ds(m, 1)].rearrange("a (c n) l -> n a c l", c=2)[bass.ds(n, 1)]
                src = src.rearrange("n a c l -> (n a) c l").broadcast_to([P, 2, L])
                sp.dma_start(bc[odd][:], src).then_inc(bc_ld[odd], 16)

            def load_matrix(w, name, hi, lo, step, e):
                if some(step):
                    sp.wait_ge(hi, T * step)
                    sp.wait_ge(lo, T * step)
                src = t[name] if e is None else t[name][bass.ds(e, 1)].rearrange("a d h -> (a d) h")
                sp.dma_start(w_raw[w][:], src.rearrange("(k p) h -> p k h", p=P)).then_inc(raw_ld[w], 16)

            def load_up(step, e):
                load_matrix(0, "Ws1" if e is None else "W1", w1h, w1l, step, e)
                load_matrix(1, "Wsg" if e is None else "Wg", wgh, wgl, step, e)

            def load_down(step, e):
                load_matrix(2, "Ws2" if e is None else "W2", w2h, w2l, step, e)

            load_ctx(0)
            for dst, src in small:
                sp.dma_start(dst, src).then_inc(const_ld, 16)
            load_x(0)
            load_up(0, None)
            load_down(0, None)
            store_xd(0)
            load_bc(0, 0, 0)
            load_bc(0, 1, 1)
            with sp.Fori(1, DS // 2) as i:
                load_bc(0, 2 * i, 0)
                load_bc(0, 2 * i + 1, 1)
            load_x_rows(0)
            load_up(1, 0)
            with sp.Fori(0, NB - 1) as b:
                m = b + 1
                load_ctx(m)
                load_down(STEPS * b + 1, 0)
                load_x(m)
                store_xd(m)
                load_bc(m, 0, 0)
                load_bc(m, 1, 1)
                load_up(STEPS * b + 2, 1)
                load_down(STEPS * b + 2, 1)
                load_bc(m, 2, 0)
                load_up(STEPS * b + 3, 2)
                load_bc(m, 3, 1)
                with sp.Fori(0, 2) as q:
                    load_down(STEPS * b + 2 * q + 3, 2 * q + 2)
                    load_bc(m, 6 * q + 4, 0)
                    load_up(STEPS * b + 2 * q + 4, 2 * q + 3)
                    load_bc(m, 6 * q + 5, 1)
                    load_bc(m, 6 * q + 6, 0)
                    load_down(STEPS * b + 2 * q + 4, 2 * q + 3)
                    load_bc(m, 6 * q + 7, 1)
                    load_up(STEPS * b + 2 * q + 5, 2 * q + 4)
                    load_bc(m, 6 * q + 8, 0)
                    load_bc(m, 6 * q + 9, 1)
                load_down(STEPS * b + 7, 6)
                load_up(STEPS * b + 8, None)
                load_x_rows(m)
                load_down(STEPS * b + 8, None)
                load_up(STEPS * b + 9, 0)
            load_down(STEPS * (NB - 1) + 1, 0)
            with sp.Fori(0, NE - 1) as e:
                load_up(STEPS * (NB - 1) + e + 2, e + 1)
                load_down(STEPS * (NB - 1) + e + 2, e + 1)
            sp.wait_ge(acc_done, T * STEPS * NB)
            sp.dma_start(out[NB - 1].rearrange("(i p) d -> p i d", p=P), acc[:]).then_inc(out_st, 16)
            sp.wait_ge(out_st, 16 * NB)

        @block.tensor
        def _(pe):
            def three_passes(out_, lhs, rhs, sides, first, last):
                for q, (a, c) in enumerate(sides):
                    mm = pe.matmul(out_, lhs[a], rhs[c], start=first and q == 0, stop=last and q == len(sides) - 1)
                return mm

            def in_proj(m):
                pe.wait_ge(ctx_ld, 16 * (m + 1))
                for et in range(T):
                    for k in range(KM):
                        mm = pe.matmul(front_ps[et][:], in_w[:, k, et * P:(et + 1) * P], ctxT[:, k, :],
                                       start=k == 0, stop=k == KM - 1)
                    mm.then_inc(inproj_done, 1)

            def x_proj(m):
                for et in range(T):
                    pe.wait_ge(u_ready, T * m + et + 1)
                    mm = pe.matmul(ps_m[0:XP, :], xproj_w[:, et, :], u[:, et, :], start=et == 0, stop=et == T - 1)
                mm.then_inc(xp_done, 1)

            def dt_proj(m):
                pe.wait_ge(xd_ready, m + 1)
                for et in range(T):
                    pe.matmul(front_ps[et][:], dt_w[:, et * P:(et + 1) * P], xdbl[0:DR, :],
                              start=True, stop=True).then_inc(dt_done, 1)

            def y_to_rows(m):
                pe.wait_ge(y_ready, m + 1)
                for i in range(T):
                    for et in range(T):
                        mm = pe.transpose(front_ps[i][:, et * P:(et + 1) * P], yacc[:, et, i * P:(i + 1) * P], ident[:])
                    mm.then_inc(yt_done, 1)

            def x2_to_columns(m):
                for i in range(T):
                    pe.wait_ge(x2_ready, T * m + i + 1)
                    for k in range(T):
                        mm = pe.transpose(mid_ps[i][:, k * P:(k + 1) * P], st[0][:, i, k * P:(k + 1) * P], ident[:])
                    mm.then_inc(xt_done, 1)

            def router_columns(b):
                for k in range(T):
                    mm = three_passes(ps_m[:], [gw_hi[:, k, :], gw_lo[:, k, :]], [x_hi[:, k, :], x_lo[:, k, :]],
                                      ((0, 0), (0, 1), (1, 0)), k == 0, k == T - 1)
                mm.then_inc(lt_done, 1)

            def router_rows(b):
                pe.wait_ge(lt_ready, b + 1)
                for i in range(T):
                    mm = pe.matmul(ps_m[:, i * 8:i * 8 + NE], logits_T[:, i * P:(i + 1) * P], ident[0:NE, 0:NE],
                                   start=True, stop=True)
                mm.then_inc(gl_done, 1)

            def hidden(step, j):
                for w, (ps, hi, lo, done, free) in enumerate(((ps_h1, w1h, w1l, h1_done, m_done),
                                                             (ps_hg, wgh, wgl, hg_done, h_made))):
                    pe.wait_ge(hi, T * step + j + 1)
                    pe.wait_ge(lo, T * step + j + 1)
                    if j >= 2:
                        pe.wait_ge(free, T * step + j - 1)
                    for k in range(T):
                        mm = three_passes(ps[j % 2][:], [v[w][:, k, j * P:(j + 1) * P] for v in (w_hi, w_lo)],
                                          [x_hi[:, k, :], x_lo[:, k, :]], ((0, 0), (0, 1), (1, 0)), k == 0, k == T - 1)
                    mm.then_inc(done, 1)

            def expert_out(step, tiles):
                for j in range(T):
                    pe.wait_ge(hh_ready, T * step + j + 1)
                    pe.wait_ge(w2h, T * step + j + 1)
                    pe.wait_ge(w2l, T * step + j + 1)
                    for i in tiles:
                        three_passes(ps_y[i % 3][:], [h_hi[:, j, i * P:(i + 1) * P]], [w_hi[2][:, j, :], w_lo[2][:, j, :]],
                                     ((0, 0), (0, 1)), j == 0, False)
                for i in tiles:
                    for j in range(T):
                        pe.wait_ge(hl_ready, T * step + j + 1)
                        mm = pe.matmul(ps_y[i % 3][:], h_lo[:, j, i * P:(i + 1) * P], w_hi[2][:, j, :],
                                       start=False, stop=j == T - 1)
                    mm.then_inc(y_done, 1)

            def shared_step(b, m=None):
                step = STEPS * b
                if m is not None:
                    pe.wait_ge(xl_ready, T * b + 1)
                    in_proj(m)
                pe.wait_ge(xl_ready, T * (b + 1))
                hidden(step, 0)
                hidden(step, 1)
                if m is not None:
                    x_proj(m)
                hidden(step, 2)
                if m is not None:
                    dt_proj(m)
                hidden(step, 3)
                if m is not None:
                    pe.wait_ge(dt_read, T * m + 2)
                else:
                    pe.wait_ge(acc_done, T * step)
                expert_out(step, (0, 1))
                if m is not None:
                    pe.wait_ge(dt_read, T * (m + 1))
                router_columns(b)
                expert_out(step, (2,))
                router_rows(b)
                pe.wait_ge(acc_done, T * step + 1)
                expert_out(step, (3,))

            def routed_step(step):
                for j in range(T):
                    hidden(step, j)
                pe.wait_ge(acc_done, T * step)
                expert_out(step, (0, 1))
                expert_out(step, (2,))
                pe.wait_ge(acc_done, T * step + 1)
                expert_out(step, (3,))

            def last_step(b, m):
                step = STEPS * b + NE
                hidden(step, 0)
                hidden(step, 1)
                pe.wait_ge(acc_done, T * step)
                y_to_rows(m)
                hidden(step, 2)
                hidden(step, 3)
                pe.wait_ge(x1_ready, T * (m + 1))
                expert_out(step, (0, 1))
                pe.wait_ge(h_made, T * (step + 1))
                x2_to_columns(m)
                expert_out(step, (2,))
                pe.wait_ge(acc_done, T * step + 1)
                expert_out(step, (3,))

            pe.wait_ge(const_ld, 16 * NCONST)
            in_proj(0)
            pe.wait_ge(setup_v, 3)
            x_proj(0)
            dt_proj(0)
            y_to_rows(0)
            x2_to_columns(0)
            with pe.Fori(0, NB - 1) as b:
                shared_step(b, b + 1)
                routed_step(STEPS * b + 1)
                with pe.Fori(0, 2) as q:
                    routed_step(STEPS * b + 2 * q + 2)
                    routed_step(STEPS * b + 2 * q + 3)
                routed_step(STEPS * b + NE - 1)
                last_step(b, b + 1)
            shared_step(NB - 1)
            with pe.Fori(1, STEPS) as e:
                routed_step(STEPS * (NB - 1) + e)

        @block.scalar
        def _(act):
            def front_conv(m):
                if some(DS * m):
                    act.wait_ge(bmul_done, DS * m)
                for et in range(T):
                    act.wait_ge(inproj_done, T * m + et + 1)
                    act.activation(u[:, et, :], front_ps[et][:], ACT.Identity, bias=conv_b[:, et:et + 1],
                                   scale=conv_w[:, et, DC - 1:DC]).then_inc(tap0_done, 1)

            def front_tanh(m):
                if some(DS * m):
                    act.wait_ge(scan_done, DS * m)
                for et in range(T):
                    act.wait_ge(conv_done, T * (DC - 1) * m + T * (DC - 2) + et + 1)
                    act.activation(dA[0][:, et, :], u[:, et, :], ACT.Tanh, scale=0.5).then_inc(ut_done, 1)

            def front_z(m):
                act.wait_ge(zn_ready, T * (m + 1))
                if some(m):
                    act.wait_ge(acc_done, T * (STEPS * (m - 1) + 1))
                act.activation(z2[:], dA[1][:], ACT.Tanh, scale=0.5).then_inc(zt_ready, 1)

            def front_yinit(m):
                if some(T * m):
                    act.wait_ge(yt_done, T * m)
                for et in range(T):
                    act.wait_ge(u_ready, T * m + et + 1)
                    act.activation(yacc[:, et, :], u[:, et, :], ACT.Copy, scale=half_D[:, et:et + 1]).then_inc(yinit_done, 1)

            def front_xd(m):
                act.wait_ge(xp_done, m + 1)
                if some(16 * m):
                    act.wait_ge(xd_st, 16 * m)
                if some(T * m):
                    act.wait_ge(dt_done, T * m)
                act.activation(xdbl[:], ps_m[0:XP, :], ACT.Copy).then_inc(xd_ready, 1)

            def front_dt(m, tiles):
                if 0 in tiles:
                    act.wait_ge(u_ready, T * (m + 1))
                for et in tiles:
                    act.wait_ge(dt_done, T * m + et + 1)
                    act.activation(dA[0][:, et, :], front_ps[et][:], ACT.Abs, bias=dt_b[:, et:et + 1])
                    act.activation(delta[:, et, :], front_ps[et][:], ACT.Relu, bias=dt_b[:, et:et + 1]).then_inc(dt_read, 1)

            def front_exp(m):
                act.wait_ge(dt_read, T * (m + 1))
                act.activation(dA[0][:], dA[0][:], ACT.Exp, scale=-1.0).then_inc(e_ready, 1)

            def front_ln(m):
                if some(m):
                    act.wait_ge(xt_done, T * m)
                act.wait_ge(e_ready, m + 1)
                act.activation(st[0][:], dA[0][:], ACT.Ln, bias=ones[:, 0:1]).then_inc(ln_ready, 1)

            def decay(m, n, odd, et):
                if et == 0:
                    act.wait_ge(zero_done, 2 * m + 1 + odd)
                    if some(DS * m + n - 1):
                        act.wait_ge(scan_done, DS * m + n - 1)
                act.activation(dA[odd][:, et, 1:L], delta[:, et, 1:L], ACT.Exp,
                               scale=neg_A[:, et, bass.ds(n, 1)]).then_inc(da_ready, 1)

            def decays(m, half, off, count, j):
                for q in range(j * count, (j + 1) * count):
                    k = off + q // T
                    decay(m, 2 * half + k, k % 2, q % T)

            def x_high(m):
                for i in range(T):
                    act.wait_ge(xt_done, T * m + i + 1)
                    ps = mid_ps[i][:].rearrange("p (k l) -> p k l", k=T)
                    act.activation(x_hi[:, :, i * P:(i + 1) * P], ps, ACT.Copy).then_inc(xh_ready, 1)

            def router_exp(b):
                act.wait_ge(r_sub, b + 1)
                act.activation(probs[:], logits[:], ACT.Exp).then_inc(r_exp, 1)

            def router_columns(b):
                act.wait_ge(lt_done, b + 1)
                act.activation(logits_T[:], ps_m[0:NE, :], ACT.Copy).then_inc(lt_ready, 1)

            def split_hi(step, w, name, j):
                act.wait_ge(raw_ld[w], 16 * (step + 1))
                sel = (slice(None), slice(None), slice(j * P, (j + 1) * P)) if w < 2 else (slice(None), j)
                act.activation(w_hi[w][sel], w_raw[w][sel], ACT.Copy).then_inc(name, 1)

            def up(step, between=None, split=True):
                for j in range(T):
                    act.wait_ge(h1_done, T * step + j + 1)
                    if j >= 2:
                        act.wait_ge(hl_ready, T * step + j - 1)
                    act.activation(h_tmp[j % 2][:], ps_h1[j % 2][:], ACT.Tanh, scale=0.5).then_inc(t_done, 1)
                    if split:
                        split_hi(step + 1, 0, w1h, j)
                    if between:
                        between(j)
                    act.wait_ge(h_made, T * step + j + 1)
                    act.activation(h_hi[:, j, :], h_tmp[j % 2][:], ACT.Copy).then_inc(hh_ready, 1)
                    if split:
                        split_hi(step + 1, 1, wgh, j)

            def down(step):
                act.wait_ge(y_done, T * (step + 1))
                for j in range(T):
                    split_hi(step + 1, 2, w2h, j)

            def shared_step(b, m=None):
                if m is not None:
                    front_conv(m)
                    front_tanh(m)

                def between(j):
                    if j == 1:
                        front_yinit(m)
                    if j == 2:
                        front_xd(m)
                    if j == 3:
                        front_dt(m, (0, 1))

                up(STEPS * b, between if m is not None else None)
                if m is not None:
                    front_dt(m, (2, 3))
                    front_exp(m)
                router_columns(b)
                if m is not None:
                    front_ln(m)
                down(STEPS * b)
                if m is not None:
                    front_z(m)

            def routed_step(step, m, half, off, count):
                up(step, lambda j: decays(m, half, off, count, j))
                down(step)

            act.wait_ge(const_ld, 16 * NCONST)
            act.activation(gate_tanh[:], gates[:], ACT.Tanh).then_inc(setup_a, 1)
            act.activation(neg_A[:], neg_A[:], ACT.Exp).then_inc(setup_a, 1)
            front_conv(0)
            front_tanh(0)
            act.wait_ge(setup_v, 3)
            front_yinit(0)
            front_xd(0)
            front_dt(0, range(T))
            front_exp(0)
            act.wait_ge(setup_v, 3)
            front_ln(0)
            front_z(0)
            for n in range(2):
                for et in range(T):
                    decay(0, n, n, et)
            for j in range(T):
                split_hi(0, 0, w1h, j)
                split_hi(0, 1, wgh, j)
                split_hi(0, 2, w2h, j)
            with act.Fori(1, DS // 2) as i:
                for odd in range(2):
                    for et in range(T):
                        decay(0, 2 * i + odd, odd, et)
            x_high(0)
            with act.Fori(0, NB - 1) as b:
                m = b + 1
                shared_step(b, m)

                def first_routed(j):
                    if j == 1:
                        router_exp(b)
                    decays(m, 0, 0, 2, j)

                up(STEPS * b + 1, first_routed)
                down(STEPS * b + 1)
                with act.Fori(0, 2) as q:
                    routed_step(STEPS * b + 2 * q + 2, m, 3 * q + 1, 0, 3)
                    routed_step(STEPS * b + 2 * q + 3, m, 3 * q + 1, 3, 3)
                routed_step(STEPS * b + NE - 1, m, DS // 2 - 1, 0, 2)
                up(STEPS * b + NE)
                x_high(m)
                down(STEPS * b + NE)
                act.wait_ge(acc_done, T * STEPS * (b + 1))
                act.dma_start(out[bass.ds(b, 1)].rearrange("a (i p) d -> p (a i) d", p=P), acc[:]).then_inc(out_st, 16)
                act.wait_ge(out_st, 16 * (b + 1))
            shared_step(NB - 1)
            router_exp(NB - 1)
            with act.Fori(1, NE) as e:
                up(STEPS * (NB - 1) + e)
                down(STEPS * (NB - 1) + e)
            up(STEPS * NB - 1, split=False)

        @block.vector
        def _(dve):
            def front_conv(m):
                for k in range(DC - 1):
                    back_ = DC - 1 - k
                    for et in range(T):
                        if k == 0:
                            dve.wait_ge(tap0_done, T * m + et + 1)
                        else:
                            dve.wait_ge(conv_done, T * (DC - 1) * m + T * (k - 1) + et + 1)
                        dve.scalar_tensor_tensor(out=u[:, et, back_:L], in0=front_ps[et][:, 0:L - back_],
                                                 scalar=conv_w[:, et, k:k + 1], in1=u[:, et, back_:L],
                                                 op0=ALU.mult, op1=ALU.add).then_inc(conv_done, 1)

            def front_silu(m):
                for et in range(T):
                    dve.wait_ge(ut_done, T * m + et + 1)
                    dve.scalar_tensor_tensor(out=u[:, et, :], in0=dA[0][:, et, :], scalar=1.0, in1=u[:, et, :],
                                             op0=ALU.add, op1=ALU.mult).then_inc(u_ready, 1)

            def mean_and_var(m, stat_done, var_done):
                dve.wait_ge(stat_done, T * (m + 1))
                dve.memset(pause[:], 0.0)
                for i in range(T):
                    last = dve.bn_aggr(mv[:, i, :], bn[:, i, :])
                last.then_inc(mv_done, 1)
                dve.wait_ge(mv_done, 2 * m + (1 if stat_done is zstat else 2))
                dve.tensor_scalar(var_eps[:], mv[:, :, 1], EPS, None, ALU.add).then_inc(var_done, 1)

            def front_z_stats(m):
                dve.wait_ge(xz_ld, 16 * (m + 1))
                for i in range(T):
                    dve.bn_stats(bn[:, i, :], dA[1][:, i, :]).then_inc(zstat, 1)
                mean_and_var(m, zstat, zvar)

            def front_zn(m):
                dve.wait_ge(zrstd, m + 1)
                for i in range(T):
                    dve.tensor_scalar(dA[1][:, i, :], dA[1][:, i, :], mv[:, i, 0:1], rstd[:, i:i + 1],
                                      ALU.subtract, ALU.mult).then_inc(zn_ready, 1)

            def front_z2(m):
                dve.wait_ge(zt_ready, m + 1)
                dve.scalar_tensor_tensor(out=z2[:], in0=z2[:], scalar=1.0, in1=dA[1][:],
                                         op0=ALU.add, op1=ALU.mult).then_inc(z_ready, 1)
                dve.wait_ge(z_ready, m + 1)
                dve.wait_ge(zero_done, 2 * m + 1)
                dve.memset(dA[1][:, :, 0:1], 0.0).then_inc(zero_done, 1)

            def front_carry(m):
                dve.wait_ge(e_ready, m + 1)
                if some(m):
                    dve.wait_ge(yadd_done, T * DS * m)
                dve.tensor_scalar(st[1][:], dA[0][:], 1.0, None, ALU.add).then_inc(sp_chain, 1)
                dve.wait_ge(sp_chain, 3 * m + 1)
                dve.scalar_tensor_tensor(out=st[1][:], in0=st[1][:], scalar=-1.0, in1=dA[0][:],
                                         op0=ALU.add, op1=ALU.subtract).then_inc(sp_chain, 1)

            def front_delta(m):
                dve.wait_ge(ln_ready, m + 1)
                dve.wait_ge(sp_chain, 3 * m + 2)
                dve.tensor_tensor(st[0][:], st[0][:], st[1][:], ALU.subtract).then_inc(sp_chain, 1)
                dve.wait_ge(sp_chain, 3 * m + 3)
                dve.tensor_tensor(delta[:], delta[:], st[0][:], ALU.add).then_inc(delta_ready, 1)
                dve.wait_ge(delta_ready, m + 1)
                dve.memset(dA[0][:, :, 0:1], 0.0).then_inc(zero_done, 1)
                dve.wait_ge(yinit_done, T * (m + 1))
                dve.wait_ge(xp_done, m + 1)
                dve.scalar_tensor_tensor(out=u[:], in0=delta[:], scalar=0.5, in1=u[:],
                                         op0=ALU.mult, op1=ALU.mult).then_inc(du_ready, 1)

            def bmul(m, n, odd, turn):
                N = DS * m + n
                dve.wait_ge(bc_ld[odd], 16 * turn)
                dve.wait_ge(du_ready, m + 1)
                if some(N - 1):
                    dve.wait_ge(yadd_done, T * (N - 1))
                dve.tensor_tensor(st[odd][:], u[:], bc[odd][:, 0:1, :].broadcast_to([P, T, L]),
                                  ALU.mult).then_inc(bmul_done, 1)

            def scan(m, n, odd):
                N = DS * m + n
                dve.wait_ge(bmul_done, N + 1)
                dve.wait_ge(da_ready, T * (N + 1))
                flat = [v[odd][:].rearrange("p t l -> p (t l)") for v in (dA, st)]
                dve.tensor_tensor_scan(flat[1], flat[0], flat[1], 0.0, ALU.mult, ALU.add).then_inc(scan_done, 1)

            def cmul(m, n, odd):
                dve.wait_ge(scan_done, DS * m + n + 1)
                dve.tensor_tensor(st[odd][:], st[odd][:], bc[odd][:, 1:2, :].broadcast_to([P, T, L]),
                                  ALU.mult).then_inc(cmul_done, 1)

            def states(m, half, off, count, k, places=T + 2):
                for q in range(max(k, 0) * 3 * count // places, (k + 1) * 3 * count // places):
                    n, odd = off + q // 3, (off + q // 3) % 2
                    if q % 3 == 0:
                        bmul(m, 2 * half + n, odd, DS // 2 * m + half + n // 2 + 1)
                    elif q % 3 == 1:
                        scan(m, 2 * half + n, odd)
                    else:
                        cmul(m, 2 * half + n, odd)

            def make_y(m):
                dve.wait_ge(yadd_done, T * DS * (m + 1))
                dve.wait_ge(z_ready, m + 1)
                dve.scalar_tensor_tensor(out=yacc[:], in0=yacc[:], scalar=0.5, in1=z2[:],
                                         op0=ALU.mult, op1=ALU.mult).then_inc(y_ready, 1)

            def residual(m, tiles):
                dve.wait_ge(xres_ld, 16 * (m + 1))
                for i in tiles:
                    dve.wait_ge(yt_done, T * m + i + 1)
                    dve.scalar_tensor_tensor(out=x1[:, i, :], in0=front_ps[i][:], scalar=gate_tanh[:, 0:1],
                                             in1=x_rows[:, i, :], op0=ALU.mult, op1=ALU.add).then_inc(x1_ready, 1)
                for i in tiles:
                    dve.wait_ge(x1_ready, T * m + i + 1)
                    dve.bn_stats(bn[:, i, :], x1[:, i, :]).then_inc(x2stat, 1)

            def make_x2(m):
                dve.wait_ge(x2rstd, m + 1)
                for i in range(T):
                    dve.tensor_scalar(st[0][:, i, :], x1[:, i, :], mv[:, i, 0:1], rstd[:, i:i + 1],
                                      ALU.subtract, ALU.mult).then_inc(x2_ready, 1)

            def x_low(m):
                for i in range(T):
                    dve.wait_ge(xh_ready, T * m + i + 1)
                    cols = slice(i * P, (i + 1) * P)
                    dve.tensor_tensor(x_lo[:, :, cols], mid_ps[i][:].rearrange("p (k l) -> p k l", k=T),
                                      x_hi[:, :, cols].bitcast(F32), ALU.subtract).then_inc(xl_ready, 1)

            def router(m):
                links = 11
                done = [0]

                def link(ins):
                    done[0] += 1
                    ins.then_inc(r_chain, 1)
                    dve.wait_ge(r_chain, links * m + done[0])

                def over(v):
                    return v.rearrange("p (t a) -> p t a", a=1).broadcast_to([P, T, NE])

                dve.wait_ge(gl_done, m + 1)
                ps = ps_m[:, 0:8 * T].rearrange("p (i e) -> p i e", e=8)[:, :, 0:NE]
                gb = gate_b[:].rearrange("p (a e) -> p a e", a=1).broadcast_to([P, T, NE])
                bb = biases[:].rearrange("p (a e) -> p a e", a=1).broadcast_to([P, T, NE])
                dve.tensor_tensor(logits[:], ps, gb, ALU.add).then_inc(logit_read, 1)
                dve.wait_ge(logit_read, m + 1)
                link(dve.tensor_reduce(lmax[:], logits[:], AX_X, ALU.max))
                dve.tensor_tensor(logits[:], logits[:], over(lmax[:]), ALU.subtract).then_inc(r_sub, 1)
                dve.wait_ge(r_exp, m + 1)
                link(dve.tensor_reduce(psum_[:], probs[:], AX_X, ALU.add))
                link(dve.reciprocal(psum_[:], psum_[:]))
                link(dve.tensor_tensor(probs[:], probs[:], over(psum_[:]), ALU.mult))
                link(dve.tensor_tensor(biased[:], probs[:], bb, ALU.add))
                mine = biased[:].rearrange("p t (e a) -> p t e a", a=1).broadcast_to([P, T, NE, NE])
                other = biased[:].rearrange("p t (a e) -> p t a e", a=1).broadcast_to([P, T, NE, NE])
                tie = earlier[:].rearrange("p (a e) f -> p a e f", a=1).broadcast_to([P, T, NE, NE])
                for i in range(T):
                    dve.tensor_tensor(eq[:, i], other[:, i], mine[:, i], ALU.is_equal)
                    last = dve.tensor_tensor(gt[:, i], other[:, i], mine[:, i], ALU.is_gt)
                link(last)
                for i in range(T):
                    last = dve.tensor_tensor(eq[:, i], eq[:, i], tie[:, i], ALU.mult)
                link(last)
                link(dve.tensor_tensor(gt, gt, eq, ALU.add))
                link(dve.tensor_reduce(rank[:], gt, AX_X, ALU.add))
                link(dve.scalar_tensor_tensor(out=coef[:], in0=rank[:], scalar=float(TOP_K), in1=probs[:],
                                              op0=ALU.is_lt, op1=ALU.mult))
                link(dve.tensor_reduce(psum_[:], coef[:], AX_X, ALU.add))
                dve.reciprocal(psum_[:], psum_[:]).then_inc(coef_ready, 1)
                dve.wait_ge(coef_ready, 2 * m + 1)
                dve.scalar_tensor_tensor(out=coef[:], in0=coef[:], scalar=half_tgf[:, 0:1], in1=over(psum_[:]),
                                         op0=ALU.mult, op1=ALU.mult).then_inc(coef_ready, 1)
                dve.wait_ge(coef_ready, 2 * m + 2)
                assert done[0] == links

            def split_lo(step, j):
                dve.wait_ge(w1h, T * step + j + 1)
                cols = slice(j * P, (j + 1) * P)
                dve.tensor_tensor(w_lo[0][:, :, cols], w_raw[0][:, :, cols], w_hi[0][:, :, cols].bitcast(F32),
                                  ALU.subtract).then_inc(w1l, 1)

            def step_(step, e, between=None, split=True):
                def add_out(i):
                    dve.wait_ge(y_done, T * step + i + 1)
                    if e is None:
                        scale, before = half_tgf[:, 0:1], x1
                    else:
                        dve.wait_ge(acc_done, T * step + i)
                        scale, before = coef[:, i, bass.ds(e, 1)], acc
                    dve.scalar_tensor_tensor(out=acc[:, i, :], in0=ps_y[i % 3][:], scalar=scale, in1=before[:, i, :],
                                             op0=ALU.mult, op1=ALU.add).then_inc(acc_done, 1)

                for j in range(T):
                    dve.wait_ge(t_done, T * step + j + 1)
                    dve.scalar_tensor_tensor(out=h_tmp[j % 2][:], in0=h_tmp[j % 2][:], scalar=1.0, in1=ps_h1[j % 2][:],
                                             op0=ALU.add, op1=ALU.mult).then_inc(m_done, 1)
                    if split:
                        split_lo(step + 1, j)
                    dve.wait_ge(m_done, T * step + j + 1)
                    dve.wait_ge(hg_done, T * step + j + 1)
                    dve.tensor_tensor(h_tmp[j % 2][:], h_tmp[j % 2][:], ps_hg[j % 2][:], ALU.mult).then_inc(h_made, 1)
                    if between:
                        between(j)
                add_out(0)
                add_out(1)
                if between:
                    between(T)
                add_out(2)
                add_out(3)
                if between:
                    between(T + 1)

            dve.memset(ones[:], 1.0)
            dve.memset(gw_hi[:].bitcast(F32), 0.0)
            dve.memset(gw_lo[:].bitcast(F32), 0.0)
            dve.memset(minus_half[:], -0.5).then_inc(setup_v, 1)
            dve.wait_ge(const_ld, 16 * NCONST)
            dve.wait_ge(setup_v, 1)
            dve.tensor_scalar(xproj_w[:], xproj_w[:], 0.5, None, ALU.mult).then_inc(setup_v, 1)
            dve.tensor_scalar(half_D[:], half_D[:], 0.5, None, ALU.mult).then_inc(setup_v, 1)
            dve.tensor_copy(gw_hi[:, :, 0:NE], gw_raw[:]).then_inc(setup_v, 1)
            dve.wait_ge(setup_v, 4)
            dve.tensor_tensor(gw_lo[:, :, 0:NE], gw_raw[:], gw_hi[:, :, 0:NE].bitcast(F32), ALU.subtract).then_inc(setup_v, 1)
            dve.wait_ge(setup_a, 2)
            dve.tensor_scalar(half_tgf[:], gate_tanh[:, 1:2], 0.5, None, ALU.mult).then_inc(setup_v, 1)
            dve.tensor_scalar(neg_A[:], neg_A[:], -1.0, None, ALU.mult).then_inc(setup_v, 1)
            dve.wait_ge(setup_v, 7)
            front_conv(0)
            front_silu(0)
            front_z_stats(0)
            front_zn(0)
            front_carry(0)
            front_delta(0)
            front_z2(0)
            for k in range(2):
                states(0, 0, 0, 2, k, 2)
            with dve.Fori(1, DS // 2) as i:
                for k in range(2):
                    states(0, i, 0, 2, k, 2)
            make_y(0)
            for j in range(T):
                split_lo(0, j)
            residual(0, range(T))
            mean_and_var(0, x2stat, x2var)
            make_x2(0)
            x_low(0)
            with dve.Fori(0, NB - 1) as b:
                m = b + 1
                front_conv(m)

                def front(k):
                    if k == 0:
                        front_silu(m)
                    if k == 1:
                        front_z_stats(m)
                    if k == 2:
                        front_zn(m)
                    if k == T:
                        front_carry(m)
                    if k == T + 1:
                        front_delta(m)

                def first_routed(k):
                    if k == 0:
                        front_z2(m)
                        router(b)
                    else:
                        states(m, 0, 0, 2, k - 1, T + 1)

                def last(k):
                    if k == 0:
                        make_y(m)
                    if k == 1:
                        residual(m, (0, 1))
                    if k == 2:
                        residual(m, (2, 3))
                        mean_and_var(m, x2stat, x2var)
                    if k == 3:
                        make_x2(m)
                    if k == T + 1:
                        x_low(m)

                step_(STEPS * b, None, front)
                step_(STEPS * b + 1, 0, first_routed)
                with dve.Fori(0, 2) as q:
                    step_(STEPS * b + 2 * q + 2, 2 * q + 1, lambda k: states(m, 3 * q + 1, 0, 3, k))
                    step_(STEPS * b + 2 * q + 3, 2 * q + 2, lambda k: states(m, 3 * q + 1, 3, 3, k))
                step_(STEPS * b + NE - 1, NE - 2, lambda k: states(m, DS // 2 - 1, 0, 2, k))
                step_(STEPS * b + NE, NE - 1, last)
            step_(STEPS * (NB - 1), None)
            router(NB - 1)
            with dve.Fori(0, NE - 1) as e:
                step_(STEPS * (NB - 1) + e + 1, e)
            step_(STEPS * NB - 1, NE - 1, split=False)

        @block.gpsimd
        def _(pool):
            def power(sem_var, sem_rstd, m):
                pool.wait_ge(sem_var, m + 1)
                pool.tensor_tensor(rstd[:], var_eps[:], minus_half[:], ALU.pow).then_inc(sem_rstd, 1)

            def y_add(m, n, odd, tiles=range(T)):
                N = DS * m + n
                pool.wait_ge(yinit_done, T * (m + 1))
                pool.wait_ge(cmul_done, N + 1)
                for et in tiles:
                    if some(T * N + et - T + 1):
                        pool.wait_ge(yadd_done, T * N + et - T + 1)
                    pool.tensor_tensor(yacc[:, et, :], yacc[:, et, :], st[odd][:, et, :], ALU.add).then_inc(yadd_done, 1)

            def h_low(step, j):
                pool.wait_ge(hh_ready, T * step + j + 1)
                pool.tensor_tensor(h_lo[:, j, :], h_tmp[j % 2][:], h_hi[:, j, :].bitcast(F32),
                                   ALU.subtract).then_inc(hl_ready, 1)

            def split_gate(step, j):
                pool.wait_ge(wgh, T * step + j + 1)
                cols = slice(j * P, (j + 1) * P)
                pool.tensor_tensor(w_lo[1][:, :, cols], w_raw[1][:, :, cols], w_hi[1][:, :, cols].bitcast(F32),
                                   ALU.subtract).then_inc(wgl, 1)

            def split_down(step):
                for j in range(T):
                    pool.wait_ge(w2h, T * step + j + 1)
                    pool.tensor_tensor(w_lo[2][:, j], w_raw[2][:, j], w_hi[2][:, j].bitcast(F32),
                                       ALU.subtract).then_inc(w2l, 1)

            def plain_step(step, before=None, at=None):
                for j in range(T):
                    if at == j:
                        before()
                    h_low(step, j)
                    split_gate(step + 1, j)
                split_down(step + 1)

            def two_states(step, m, n):
                for j in range(T):
                    h_low(step, j)
                    split_gate(step + 1, j)
                y_add(m, n, 0)
                split_down(step + 1)
                y_add(m, n + 1, 1)

            def three_states(step, m, n, odd):
                for j in range(T):
                    h_low(step, j)
                    if j == 2:
                        y_add(m, n, odd, (0, 1))
                    if j == 3:
                        y_add(m, n, odd, (2, 3))
                    split_gate(step + 1, j)
                y_add(m, n + 1, 1 - odd)
                split_down(step + 1)
                y_add(m, n + 2, odd)

            pool.wait_ge(setup_v, 1)
            power(zvar, zrstd, 0)
            y_add(0, 0, 0)
            y_add(0, 1, 1)
            with pool.Fori(1, DS // 2) as i:
                y_add(0, 2 * i, 0)
                y_add(0, 2 * i + 1, 1)
            for j in range(T):
                split_gate(0, j)
            power(x2var, x2rstd, 0)
            split_down(0)
            with pool.Fori(0, NB - 1) as b:
                m = b + 1
                plain_step(STEPS * b, lambda: power(zvar, zrstd, m), 2)
                two_states(STEPS * b + 1, m, 0)
                with pool.Fori(0, 2) as q:
                    three_states(STEPS * b + 2 * q + 2, m, 6 * q + 2, 0)
                    three_states(STEPS * b + 2 * q + 3, m, 6 * q + 5, 1)
                two_states(STEPS * b + NE - 1, m, DS - 2)
                plain_step(STEPS * b + NE, lambda: power(x2var, x2rstd, m), 3)
            with pool.Fori(0, NE) as e:
                plain_step(STEPS * (NB - 1) + e)
            for j in range(T):
                h_low(STEPS * NB - 1, j)


def kernel(**inputs):
    import numpy as np
    import concourse.bacc as bacc
    from concourse.bass_utils import run_bass_kernel_spmd

    g = {k.replace("L0_xattn_", "").replace("L0_ffn_", ""): np.asarray(v) for k, v in inputs.items()}
    ne = g["W1"].shape[0]

    def columns(v):
        return v.reshape(-1, P).T

    arrays = {
        "x": g["x"], "ctxT": g["ctx_1024"].transpose(0, 2, 1), "g_xattn": g["g_xattn"], "g_ffn": g["g_ffn"],
        "in_wT": g["in_proj_w"].T, "conv_w": g["conv_w"], "conv_b": columns(g["conv_b"]), "xproj_wT": g["x_proj_w"].T,
        "dt_wT": g["dt_proj_w"].T, "dt_b": columns(g["dt_proj_b"]), "A_log": g["A_log"], "D": columns(g["D"]),
        "W1": g["W1"], "Wg": g["Wg"], "W2": g["W2"], "Ws1": g["Ws1"], "Wsg": g["Wsg"], "Ws2": g["Ws2"],
        "gate_w": g["gate_w"], "gate_b": g["gate_b"], "biases": g["biases"],
        "ident": np.eye(P, dtype=np.float32), "earlier": np.tril(np.ones((ne, ne), np.float32), -1).reshape(-1),
    }
    nc = bacc.Bacc("TRN2", target_bir_lowering=False, num_devices=1)
    fed, args = {}, {}
    for name in NAMES:
        a = np.ascontiguousarray(arrays[name])
        fed[f"in_{name}_dram"] = a
        args[name] = nc.dram_tensor(f"in_{name}_dram", a.shape, mybir.dt.from_np(a.dtype), kind="ExternalInput").ap()
    out = nc.dram_tensor("out_dram", g["x"].shape, F32, kind="ExternalOutput").ap()
    gated_block(nc, args, out)
    return run_bass_kernel_spmd(nc, [fed], core_ids=[0]).results[0]["out_dram"]
```

```python
from contextlib import ExitStack

import concourse.bass as bass
from concourse import mybir

F32 = mybir.dt.float32
F32R = mybir.dt.float32r
ALU = mybir.AluOpType
ACT = mybir.ActivationFunctionType
AX_X = mybir.AxisListType.X

P = 128
NAMES = ["x", "ctxT", "g_xattn", "g_ffn", "in_wT", "conv_w", "conv_b", "xproj_wT", "dt_wT", "dt_b", "A_log", "D",
         "W1", "Wg", "W2", "Ws1", "Wsg", "Ws2", "gate_w", "gate_b", "biases", "ident", "earlier"]


def gated_block(nc, t, out):
    NB, L, DI = t["x"].shape
    DM = t["ctxT"].shape[1]
    NE = t["W1"].shape[0]
    DS = t["A_log"].shape[1]
    DC = t["conv_w"].shape[1]
    DR = t["dt_wT"].shape[0]
    XP = DR + 2 * DS
    TOP_K = 3
    EPS = 1e-5
    T = DI // P
    KM = DM // P
    STEPS = NE + 1
    assert L == DI and t["W1"].shape[1:] == (DI, DI)
    assert DS == 16 and NE == 7 and NB >= 3

    xd_dram = nc.dram_tensor("xd_scratch", (NB, 2 * DS, L), F32, kind="Internal").ap()
    xin_dram = nc.dram_tensor("xin_scratch", (NB, P, T, L), F32, kind="Internal").ap()

    with ExitStack() as ctx:
        def sb(name, shape, dt=F32):
            return ctx.enter_context(nc.sbuf_tensor(name, shape, dt))

        def sem(name):
            return ctx.enter_context(nc.semaphore(name))

        in_w = sb("in_w", [P, KM, DI])
        xproj_w = sb("xproj_w", [P, T, XP])
        dt_w = sb("dt_w", [DR, DI])
        conv_w = sb("conv_w", [P, T, DC])
        conv_b = sb("conv_b", [P, T])
        dt_b = sb("dt_b", [P, T])
        neg_A = sb("neg_A", [P, T, DS])
        half_D = sb("half_D", [P, T])
        gates = sb("gates", [P, 2])
        gate_tanh = sb("gate_tanh", [P, 2])
        half_tgf = sb("half_tgf", [P, 1])
        ones = sb("ones", [P, 1])
        minus_half = sb("minus_half", [P, T])
        gw_raw = sb("gw_raw", [P, T, NE])
        gw_hi = sb("gw_hi", [P, T, P], F32R)
        gw_lo = sb("gw_lo", [P, T, P], F32R)
        gate_b = sb("gate_b", [P, NE])
        biases = sb("biases", [P, NE])
        ident = sb("ident", [P, P])
        earlier = sb("earlier", [P, NE, NE])

        ctxT = sb("ctxT", [P, KM, L])
        u = sb("u", [P, T, L])
        delta = sb("delta", [P, T, L])
        yacc = sb("yacc", [P, T, L])
        z2 = sb("z2", [P, T, L])
        x1 = z2
        x_rows = delta
        xdbl = sb("xdbl", [XP, L])
        logits_T = xdbl[0:NE]
        bc = [sb(f"bc{i}", [P, 2, L]) for i in range(2)]
        dA = [sb(f"dA{i}", [P, T, L]) for i in range(2)]
        st = [sb(f"st{i}", [P, T, L]) for i in range(2)]
        gt, eq = (st[1][:, i, 0:T * NE * NE].rearrange("p (t a e) -> p t a e", t=T, a=NE) for i in range(2))
        bn = sb("bn", [P, T, 6])
        mv = sb("mv", [P, T, 2])
        var_eps = sb("var_eps", [P, T])
        rstd = sb("rstd", [P, T])

        acc = sb("acc", [P, T, DI])
        x_hi = sb("x_hi", [P, T, L], F32R)
        x_lo = sb("x_lo", [P, T, L], F32R)
        h_tmp = [sb(f"h_tmp{i}", [P, L]) for i in range(2)]
        h_hi = sb("h_hi", [P, T, L], F32R)
        h_lo = sb("h_lo", [P, T, L], F32R)
        w_raw = [sb(f"w{n}_raw", [P, T, DI]) for n in "1g2"]
        w_hi = [sb(f"w{n}_hi", [P, T, DI], F32R) for n in "1g2"]
        w_lo = [sb(f"w{n}_lo", [P, T, DI], F32R) for n in "1g2"]
        logits = sb("logits", [P, T, NE])
        lmax = sb("lmax", [P, T])
        probs = sb("probs", [P, T, NE])
        psum_ = sb("psum_", [P, T])
        biased = sb("biased", [P, T, NE])
        pause = sb("pause", [P, 1])
        rank = sb("rank", [P, T, NE])
        coef = sb("coef", [P, T, NE])

        first_bc = [bc[0][:], bc[1][:], h_hi[:, 0:2].bitcast(F32), h_hi[:, 2:4].bitcast(F32)]
        first_hc = acc
        next_ctxT = acc[:, 0:KM]

        ps_h1 = [ctx.enter_context(nc.psum_tensor(f"ps_h1{i}", [P, L], F32)) for i in range(2)]
        ps_hg = [ctx.enter_context(nc.psum_tensor(f"ps_hg{i}", [P, L], F32)) for i in range(2)]
        ps_y = [ctx.enter_context(nc.psum_tensor(f"ps_y{i}", [P, L], F32)) for i in range(3)]
        ps_m = ctx.enter_context(nc.psum_tensor("ps_m", [P, L], F32))
        front_ps = [*ps_y, ps_m]
        dt_ps = [ps_m, ps_y[2], ps_h1[0], ps_hg[0]]
        mid_ps = [ps_h1[0], ps_hg[0], ps_h1[1], ps_hg[1]]

        const_ld = sem("const_ld")
        setup_v = sem("setup_v")
        setup_a = sem("setup_a")
        ctx_ld = sem("ctx_ld")
        next_ctx_ld = sem("next_ctx_ld")
        xz_ld = sem("xz_ld")
        xres_ld = sem("xres_ld")
        bc_ld0 = sem("bc_ld0")
        bc_ld1 = sem("bc_ld1")
        bc_ld2 = sem("bc_ld2")
        bc_ld3 = sem("bc_ld3")
        in_w_ld = sem("in_w_ld")
        warm = sem("warm")
        in_staged = sem("in_staged")
        xin_st = sem("xin_st")
        xin_ld = sem("xin_ld")
        hc_ready = sem("hc_ready")
        last_hc_ready = sem("last_hc_ready")
        xd_st = sem("xd_st")
        out_st = sem("out_st")
        raw_ld0 = sem("raw_ld0")
        raw_ld1 = sem("raw_ld1")
        raw_ld2 = sem("raw_ld2")
        inproj_done = sem("inproj_done")
        tap0_done = sem("tap0_done")
        conv_done = sem("conv_done")
        ut_done = sem("ut_done")
        u_ready = sem("u_ready")
        xp_done = sem("xp_done")
        xd_ready = sem("xd_ready")
        yinit_done = sem("yinit_done")
        dt_done = sem("dt_done")
        dt_read = sem("dt_read")
        e_ready = sem("e_ready")
        ln_ready = sem("ln_ready")
        carry1 = sem("carry1")
        carry2 = sem("carry2")
        carry3 = sem("carry3")
        delta_ready = sem("delta_ready")
        du_ready = sem("du_ready")
        zstat = sem("zstat")
        zvar = sem("zvar")
        mv_done = sem("mv_done")
        zrstd = sem("zrstd")
        zn_ready = sem("zn_ready")
        zt_ready = sem("zt_ready")
        z_ready = sem("z_ready")
        zero_done = sem("zero_done")
        da_ready = sem("da_ready")
        bmul_done = sem("bmul_done")
        scan_done = sem("scan_done")
        cmul_done = sem("cmul_done")
        yadd_done = sem("yadd_done")
        y_ready = sem("y_ready")
        yt_done = sem("yt_done")
        x1_ready = sem("x1_ready")
        x2stat = sem("x2stat")
        x2var = sem("x2var")
        x2rstd = sem("x2rstd")
        x2_ready = sem("x2_ready")
        xt_done = sem("xt_done")
        xh_ready = sem("xh_ready")
        xl_ready = sem("xl_ready")
        lt_done = sem("lt_done")
        lt_ready = sem("lt_ready")
        gl_done = sem("gl_done")
        logit_read = sem("logit_read")
        r_chain = sem("r_chain")
        r_sub = sem("r_sub")
        r_exp = sem("r_exp")
        coef_ready = sem("coef_ready")
        h1_done = sem("h1_done")
        hg_done = sem("hg_done")
        t_done = sem("t_done")
        m_done = sem("m_done")
        h_made = sem("h_made")
        hh_ready = sem("hh_ready")
        hl_ready = sem("hl_ready")
        y_done = sem("y_done")
        acc_done = sem("acc_done")
        w1h = sem("w1h")
        wgh = sem("wgh")
        w2h = sem("w2h")
        w1l = sem("w1l")
        wgl = sem("wgl")
        w2l = sem("w2l")
        raw_ld = [raw_ld0, raw_ld1, raw_ld2]
        bc_ld = [bc_ld0, bc_ld1, bc_ld2, bc_ld3]
        RING = len(bc_ld)
        WARM_START, WARM_CONV, WARM_NORM = 9, 17, 29
        NCONST = 14

        def some(count):
            return not (isinstance(count, int) and count <= 0)

        block = ctx.enter_context(nc.Block())

        def conv_in(m, et):
            return st[1][:, et, :] if some(m) else front_ps[et][:]

        def bcast(a, n):
            return a.rearrange("(a n) -> a n", a=1).broadcast_to([P, n])

        @block.sync
        def _(sp):
            small = [
                (dt_b[:], t["dt_b"]),
                (neg_A[:], t["A_log"].rearrange("(t p) c -> p t c", p=P)),
                (gw_raw[:, :, 0:NE], t["gate_w"].rearrange("(t p) c -> p t c", p=P)),
                (gate_b[:], bcast(t["gate_b"], NE)),
                (biases[:], bcast(t["biases"], NE)),
                (ident[:], t["ident"]),
                (earlier[:].rearrange("p a b -> p (a b)"), bcast(t["earlier"], NE * NE)),
            ]

            def load_ctx(m):
                into, loaded = (next_ctxT, next_ctx_ld) if m == 1 else (ctxT[:], ctx_ld)
                if m > 1:
                    sp.wait_ge(inproj_done, T * (1 if m == 2 else m))
                sp.dma_start(into, t["ctxT"][bass.ds(m, 1)].rearrange("a (k p) l -> p (a k) l", p=P)).then_inc(loaded, 16)

            def load_xin(m):
                sp.wait_ge(yadd_done, T * DS * m)
                sp.dma_start(st[1][:], xin_dram[bass.ds(m, 1)].rearrange("a p t l -> p (a t) l")).then_inc(xin_ld, 16)

            def load_x(m):
                if some(m):
                    sp.wait_ge(scan_done, DS * m)
                sp.dma_start(dA[1][:], t["x"][bass.ds(m, 1)].rearrange("a (i p) d -> p (a i) d", p=P)).then_inc(xz_ld, 16)

            def load_x_rows(m):
                sp.wait_ge(da_ready, T * DS * (m + 1))
                sp.dma_start(x_rows[:], t["x"][bass.ds(m, 1)].rearrange("a (i p) d -> p (a i) d", p=P)).then_inc(xres_ld, 16)

            def store_xd(m):
                sp.wait_ge(xd_ready, m + 1)
                sp.dma_start(xd_dram[bass.ds(m, 1)].rearrange("a r l -> (a r) l"), xdbl[DR:XP, :]).then_inc(xd_st, 16)

            def load_bc(m, n, odd):
                if isinstance(n, int) and n < 2:
                    sp.wait_ge(xd_st, 16 * (m + 1))
                else:
                    sp.wait_ge(cmul_done, DS * (m - 1) + n - 1)
                src = xd_dram[bass.ds(m, 1)].rearrange("a (c n) l -> n a c l", c=2)[bass.ds(n, 1)]
                src = src.rearrange("n a c l -> (n a) c l").broadcast_to([P, 2, L])
                sp.dma_start(bc[odd][:], src).then_inc(bc_ld[odd], 16)

            def load_matrix(w, name, hi, lo, step, e):
                if some(step):
                    sp.wait_ge(hi, T * step)
                    sp.wait_ge(lo, T * step)
                src = t[name] if e is None else t[name][bass.ds(e, 1)].rearrange("a d h -> (a d) h")
                sp.dma_start(w_raw[w][:], src.rearrange("(k p) h -> p k h", p=P)).then_inc(raw_ld[w], 16)

            def load_up(step, e):
                load_matrix(0, "Ws1" if e is None else "W1", w1h, w1l, step, e)
                load_matrix(1, "Wsg" if e is None else "Wg", wgh, wgl, step, e)

            def load_down(step, e):
                load_matrix(2, "Ws2" if e is None else "W2", w2h, w2l, step, e)

            def load_first_bc(n, k):
                if isinstance(n, int) and n < RING:
                    sp.wait_ge(xd_st, 16)
                else:
                    sp.wait_ge(hc_ready, T * (n + 1 - RING))
                src = xd_dram[0].rearrange("(c n) l -> n c l", c=2)[bass.ds(n, 1)].broadcast_to([P, 2, L])
                sp.dma_start(first_bc[k], src).then_inc(bc_ld[k], 16)

            load_ctx(0)
            for dst, src in small:
                sp.dma_start(dst, src).then_inc(const_ld, 16)
            load_ctx(1)
            load_x(0)
            load_up(0, None)
            load_down(0, None)
            load_ctx(2)
            store_xd(0)
            for k in range(RING):
                load_first_bc(k, k)
            for m in range(3, NB):
                load_ctx(m)
                for k in range(RING):
                    load_first_bc(RING * (m - 2) + k, k)
            with sp.Fori(NB - 2, DS // RING) as i:
                for k in range(RING):
                    load_first_bc(RING * i + k, k)
            load_x_rows(0)
            sp.wait_ge(xin_st, 16 * (NB - 1))
            with sp.Fori(0, NB - 1) as b:
                m = b + 1
                load_xin(m)
                load_up(STEPS * b + 1, 0)
                load_x(m)
                load_down(STEPS * b + 1, 0)
                store_xd(m)
                load_bc(m, 0, 0)
                load_bc(m, 1, 1)
                load_up(STEPS * b + 2, 1)
                load_down(STEPS * b + 2, 1)
                load_up(STEPS * b + 3, 2)
                load_bc(m, 2, 0)
                with sp.Fori(0, 2) as q:
                    load_down(STEPS * b + 2 * q + 3, 2 * q + 2)
                    load_bc(m, 6 * q + 3, 1)
                    load_up(STEPS * b + 2 * q + 4, 2 * q + 3)
                    load_bc(m, 6 * q + 4, 0)
                    load_bc(m, 6 * q + 5, 1)
                    load_down(STEPS * b + 2 * q + 4, 2 * q + 3)
                    load_bc(m, 6 * q + 6, 0)
                    load_up(STEPS * b + 2 * q + 5, 2 * q + 4)
                    load_bc(m, 6 * q + 7, 1)
                    load_bc(m, 6 * q + 8, 0)
                load_down(STEPS * b + 7, 6)
                load_bc(m, DS - 1, 1)
                load_up(STEPS * b + 8, None)
                load_x_rows(m)
                load_down(STEPS * b + 8, None)
            load_up(STEPS * (NB - 1) + 1, 0)
            load_down(STEPS * (NB - 1) + 1, 0)
            with sp.Fori(0, NE - 1) as e:
                load_up(STEPS * (NB - 1) + e + 2, e + 1)
                load_down(STEPS * (NB - 1) + e + 2, e + 1)
            for i in range(T):
                sp.wait_ge(acc_done, T * (STEPS * NB - 1) + i + 1)
                sp.dma_start(out[NB - 1, i * P:(i + 1) * P], acc[:, i, :]).then_inc(out_st, 16)
            sp.wait_ge(out_st, 16 * (NB - 1 + T))

        @block.tensor
        def _(pe):
            def three_passes(out_, lhs, rhs, sides, first, last):
                for q, (a, c) in enumerate(sides):
                    mm = pe.matmul(out_, lhs[a], rhs[c], start=first and q == 0, stop=last and q == len(sides) - 1)
                return mm

            def keep_warm(count):
                for _ in range(count):
                    pe.matmul(mid_ps[0][:], gw_hi[:, 0, :], gw_hi[:].rearrange("p k e -> p (k e)"),
                              start=True, stop=True).then_inc(warm, 1)

            def in_proj(m, et):
                context, banks = (next_ctxT, mid_ps) if isinstance(m, int) and m == 1 else (ctxT, front_ps)
                for k in range(KM):
                    mm = pe.matmul(banks[et][:], in_w[:, k, et * P:(et + 1) * P], context[:, k, :],
                                   start=k == 0, stop=k == KM - 1)
                mm.then_inc(inproj_done, 1)

            def x_proj(m):
                for et in range(T):
                    pe.wait_ge(u_ready, T * m + et + 1)
                    mm = pe.matmul(ps_m[0:XP, :], xproj_w[:, et, :], u[:, et, :], start=et == 0, stop=et == T - 1)
                mm.then_inc(xp_done, 1)

            def dt_proj(m):
                pe.wait_ge(xd_ready, m + 1)
                for et in range(T):
                    pe.matmul(dt_ps[et][:], dt_w[:, et * P:(et + 1) * P], xdbl[0:DR, :],
                              start=True, stop=True).then_inc(dt_done, 1)

            def y_to_rows(m):
                pe.wait_ge(y_ready, m + 1)
                for i in range(T):
                    for et in range(T):
                        mm = pe.transpose(front_ps[i][:, et * P:(et + 1) * P], yacc[:, et, i * P:(i + 1) * P], ident[:])
                    mm.then_inc(yt_done, 1)

            def first_y(n):
                for et in range(T):
                    pe.wait_ge(hc_ready, T * n + et + 1)
                    pe.matmul(mid_ps[et][:], ident[:], first_hc[:, et, :], start=False, stop=False).then_inc(yadd_done, 1)

            def first_y_last():
                for et in range(T):
                    pe.wait_ge(last_hc_ready, et + 1)
                    pe.matmul(mid_ps[et][:], ident[:], st[1][:, et, :], start=False, stop=True).then_inc(yadd_done, 1)

            def x2_to_columns(m):
                for i in range(T):
                    pe.wait_ge(x2_ready, T * m + i + 1)
                    for k in range(T):
                        mm = pe.transpose(mid_ps[i][:, k * P:(k + 1) * P], st[0][:, i, k * P:(k + 1) * P], ident[:])
                    mm.then_inc(xt_done, 1)

            def router_columns(b):
                for k in range(T):
                    mm = three_passes(ps_m[:], [gw_hi[:, k, :], gw_lo[:, k, :]], [x_hi[:, k, :], x_lo[:, k, :]],
                                      ((0, 0), (0, 1), (1, 0)), k == 0, k == T - 1)
                mm.then_inc(lt_done, 1)

            def router_rows(b):
                pe.wait_ge(lt_ready, b + 1)
                for i in range(T):
                    mm = pe.matmul(ps_m[:, i * 8:i * 8 + NE], logits_T[:, i * P:(i + 1) * P], ident[0:NE, 0:NE],
                                   start=True, stop=True)
                mm.then_inc(gl_done, 1)

            def hidden(step, j):
                for w, (ps, hi, lo, done, free) in enumerate(((ps_h1, w1h, w1l, h1_done, m_done),
                                                             (ps_hg, wgh, wgl, hg_done, h_made))):
                    pe.wait_ge(hi, T * step + j + 1)
                    pe.wait_ge(lo, T * step + j + 1)
                    if j >= 2:
                        pe.wait_ge(free, T * step + j - 1)
                    for k in range(T):
                        mm = three_passes(ps[j % 2][:], [v[w][:, k, j * P:(j + 1) * P] for v in (w_hi, w_lo)],
                                          [x_hi[:, k, :], x_lo[:, k, :]], ((0, 0), (0, 1), (1, 0)), k == 0, k == T - 1)
                    mm.then_inc(done, 1)

            def expert_out(step, tiles):
                for j in range(T):
                    pe.wait_ge(hh_ready, T * step + j + 1)
                    pe.wait_ge(w2h, T * step + j + 1)
                    pe.wait_ge(w2l, T * step + j + 1)
                    for i in tiles:
                        three_passes(ps_y[i % 3][:], [h_hi[:, j, i * P:(i + 1) * P]], [w_hi[2][:, j, :], w_lo[2][:, j, :]],
                                     ((0, 0), (0, 1)), j == 0, False)
                for i in tiles:
                    for j in range(T):
                        pe.wait_ge(hl_ready, T * step + j + 1)
                        mm = pe.matmul(ps_y[i % 3][:], h_lo[:, j, i * P:(i + 1) * P], w_hi[2][:, j, :],
                                       start=False, stop=j == T - 1)
                    mm.then_inc(y_done, 1)

            def shared_step(b, m=None):
                step = STEPS * b
                pe.wait_ge(xl_ready, T * (b + 1))
                hidden(step, 0)
                hidden(step, 1)
                hidden(step, 2)
                if m is not None:
                    x_proj(m)
                hidden(step, 3)
                if m is not None:
                    pe.wait_ge(h_made, T * step + 3)
                    dt_proj(m)
                expert_out(step, (0, 1))
                if m is not None:
                    pe.wait_ge(dt_read, 2 * T * m + 2)
                router_columns(b)
                if m is not None:
                    pe.wait_ge(dt_read, 2 * T * m + 4)
                expert_out(step, (2,))
                router_rows(b)
                if m is not None:
                    pe.wait_ge(dt_read, 2 * T * (m + 1))
                pe.wait_ge(acc_done, T * step + 1)
                expert_out(step, (3,))

            def routed_step(step):
                for j in range(T):
                    hidden(step, j)
                pe.wait_ge(acc_done, T * step)
                expert_out(step, (0, 1))
                expert_out(step, (2,))
                pe.wait_ge(acc_done, T * step + 1)
                expert_out(step, (3,))

            def last_step(b, m):
                step = STEPS * b + NE
                hidden(step, 0)
                hidden(step, 1)
                pe.wait_ge(acc_done, T * step)
                y_to_rows(m)
                hidden(step, 2)
                hidden(step, 3)
                pe.wait_ge(x1_ready, T * (m + 1))
                expert_out(step, (0, 1))
                pe.wait_ge(h_made, T * (step + 1))
                x2_to_columns(m)
                expert_out(step, (2,))
                pe.wait_ge(acc_done, T * step + 1)
                expert_out(step, (3,))

            pe.wait_ge(setup_v, 1)
            keep_warm(WARM_START)
            pe.wait_ge(in_w_ld, 16)
            pe.wait_ge(ctx_ld, 16)
            for et in range(T):
                in_proj(0, et)
            pe.wait_ge(next_ctx_ld, 16)
            for et in range(T):
                in_proj(1, et)
            pe.wait_ge(const_ld, 16 * NCONST)
            pe.wait_ge(setup_v, 7)
            pe.wait_ge(in_staged, 1)
            keep_warm(WARM_CONV)
            x_proj(0)
            pe.wait_ge(in_staged, T)
            dt_proj(0)
            pe.wait_ge(dt_read, 2 * T)
            pe.wait_ge(yinit_done, T)
            for et in range(T):
                pe.matmul(mid_ps[et][:], ident[:], yacc[:, et, :], start=True, stop=False)
            pe.wait_ge(ctx_ld, 16 * 2)
            for et in range(T):
                in_proj(2, et)
            first_y(0)
            with pe.Fori(1, T) as n:
                first_y(n)
            for m in range(3, NB):
                for k in range(T):
                    first_y(T * (m - 2) + k)
                    pe.wait_ge(ctx_ld, 16 * m)
                    pe.wait_ge(in_staged, T * (m - 2) + k + 1)
                    in_proj(m, k)
            with pe.Fori(T * (NB - 2), DS - 1) as n:
                first_y(n)
            first_y_last()
            y_to_rows(0)
            keep_warm(WARM_NORM)
            x2_to_columns(0)
            with pe.Fori(0, NB - 1) as b:
                shared_step(b, b + 1)
                routed_step(STEPS * b + 1)
                with pe.Fori(0, 2) as q:
                    routed_step(STEPS * b + 2 * q + 2)
                    routed_step(STEPS * b + 2 * q + 3)
                routed_step(STEPS * b + NE - 1)
                last_step(b, b + 1)
            shared_step(NB - 1)
            with pe.Fori(1, STEPS) as e:
                routed_step(STEPS * (NB - 1) + e)

        @block.scalar
        def _(act):
            small = [
                (conv_w[:], t["conv_w"].rearrange("(t p) c -> p t c", p=P)),
                (conv_b[:], t["conv_b"]),
                (xproj_w[:], t["xproj_wT"].rearrange("(t p) c -> p t c", p=P)),
                (dt_w[:], t["dt_wT"]),
                (half_D[:], t["D"]),
                (gates[:, 0:1], bcast(t["g_xattn"], 1)),
                (gates[:, 1:2], bcast(t["g_ffn"], 1)),
            ]

            def front_conv(m):
                if some(m):
                    act.wait_ge(bmul_done, DS * m)
                if some(m):
                    act.wait_ge(xin_ld, 16 * m)
                for et in range(T):
                    if not some(m):
                        act.wait_ge(inproj_done, et + 1)
                    act.activation(u[:, et, :], conv_in(m, et), ACT.Identity, bias=conv_b[:, et:et + 1],
                                   scale=conv_w[:, et, DC - 1:DC]).then_inc(tap0_done, 1)

            def front_tanh(m):
                if some(m):
                    act.wait_ge(scan_done, DS * m)
                for et in range(T):
                    act.wait_ge(conv_done, T * (DC - 1) * m + T * (DC - 2) + et + 1)
                    act.activation(dA[0][:, et, :], u[:, et, :], ACT.Tanh, scale=0.5).then_inc(ut_done, 1)

            def front_z(m):
                act.wait_ge(zn_ready, T * (m + 1))
                if some(m):
                    act.wait_ge(delta_ready, T * (m + 1))
                act.activation(st[1][:], dA[1][:], ACT.Tanh, scale=0.5).then_inc(zt_ready, 1)

            def front_yinit(m):
                if some(m):
                    act.wait_ge(yt_done, T * m)
                for et in range(T):
                    act.wait_ge(u_ready, T * m + et + 1)
                    act.activation(yacc[:, et, :], u[:, et, :], ACT.Copy, scale=half_D[:, et:et + 1]).then_inc(yinit_done, 1)

            def front_xd(m):
                act.wait_ge(xp_done, m + 1)
                if some(m):
                    act.wait_ge(xd_st, 16 * m)
                    act.wait_ge(dt_done, T * m)
                act.activation(xdbl[:], ps_m[0:XP, :], ACT.Copy).then_inc(xd_ready, 1)

            def front_dt(m, tiles):
                if 0 in tiles:
                    act.wait_ge(u_ready, T * (m + 1))
                for et in tiles:
                    act.wait_ge(dt_done, T * m + et + 1)
                    act.activation(dA[0][:, et, :], dt_ps[et][:], ACT.Abs, bias=dt_b[:, et:et + 1]).then_inc(dt_read, 1)
                    act.activation(delta[:, et, :], dt_ps[et][:], ACT.Relu, bias=dt_b[:, et:et + 1]).then_inc(dt_read, 1)
                    act.wait_ge(dt_read, 2 * T * m + 2 * et + 1)
                    act.activation(dA[0][:, et, :], dA[0][:, et, :], ACT.Exp, scale=-1.0).then_inc(e_ready, 1)

            def front_ln(m, tiles):
                if 0 in tiles:
                    if some(m):
                        act.wait_ge(xt_done, T * m)
                    else:
                        act.wait_ge(xin_st, 16)
                for et in tiles:
                    act.wait_ge(e_ready, T * m + et + 1)
                    act.activation(st[0][:, et, :], dA[0][:, et, :], ACT.Ln, bias=ones[:, 0:1]).then_inc(ln_ready, 1)

            def decay(m, n, odd, et):
                if et == 0:
                    act.wait_ge(zero_done, 2 * m + 1 + odd)
                    if some(DS * m + n - 1):
                        act.wait_ge(scan_done, DS * m + n - 1)
                act.activation(dA[odd][:, et, 1:L], delta[:, et, 1:L], ACT.Exp,
                               scale=neg_A[:, et, bass.ds(n, 1)]).then_inc(da_ready, 1)

            def decays(m, half, off, count, j):
                for q in range(j * count, (j + 1) * count):
                    k = off + q // T
                    decay(m, 2 * half + k, k % 2, q % T)

            def stage(m, et):
                first = isinstance(m, int) and m == 1
                banks, staged = (mid_ps, st[0]) if first else (front_ps, yacc)
                if et == 0 and some(m - 1):
                    act.wait_ge(xin_st, 16 * (m - 1))
                act.wait_ge(inproj_done, T * m + et + 1)
                act.activation(staged[:, et, :], banks[et][:], ACT.Copy).then_inc(in_staged, 1)
                if et == T - 1:
                    act.wait_ge(in_staged, T * m)
                    act.dma_start(xin_dram[bass.ds(m, 1)].rearrange("a p t l -> p (a t) l"), staged[:]).then_inc(xin_st, 16)

            def x_high(m):
                for i in range(T):
                    act.wait_ge(xt_done, T * m + i + 1)
                    ps = mid_ps[i][:].rearrange("p (k l) -> p k l", k=T)
                    act.activation(x_hi[:, :, i * P:(i + 1) * P], ps, ACT.Copy).then_inc(xh_ready, 1)

            def router_exp(b):
                act.wait_ge(r_sub, b + 1)
                act.activation(probs[:], logits[:], ACT.Exp).then_inc(r_exp, 1)

            def router_columns(b):
                act.wait_ge(lt_done, b + 1)
                act.activation(logits_T[:], ps_m[0:NE, :], ACT.Copy).then_inc(lt_ready, 1)

            def split_hi(step, w, name, j):
                act.wait_ge(raw_ld[w], 16 * (step + 1))
                sel = (slice(None), slice(None), slice(j * P, (j + 1) * P)) if w < 2 else (slice(None), j)
                act.activation(w_hi[w][sel], w_raw[w][sel], ACT.Copy).then_inc(name, 1)

            def up(step, between=None, split=True, after=None):
                for j in range(T):
                    act.wait_ge(h1_done, T * step + j + 1)
                    if j >= 2:
                        act.wait_ge(hl_ready, T * step + j - 1)
                    act.activation(h_tmp[j % 2][:], ps_h1[j % 2][:], ACT.Tanh, scale=0.5).then_inc(t_done, 1)
                    if split:
                        split_hi(step + 1, 0, w1h, j)
                    if between:
                        between(j)
                    act.wait_ge(h_made, T * step + j + 1)
                    act.activation(h_hi[:, j, :], h_tmp[j % 2][:], ACT.Copy).then_inc(hh_ready, 1)
                    if split:
                        split_hi(step + 1, 1, wgh, j)
                    if after:
                        after(j)

            def split_down(step, tiles=range(T)):
                for j in tiles:
                    split_hi(step, 2, w2h, j)

            def down(step):
                act.wait_ge(y_done, T * (step + 1))
                split_down(step + 1)

            def shared_step(b, m=None):
                if m is not None:
                    front_conv(m)

                def between(j):
                    if j < 2:
                        split_down(STEPS * b, (2 * j, 2 * j + 1))
                    if m is None:
                        return
                    if j == 2:
                        front_yinit(m)
                        front_xd(m)

                def after(j):
                    if j == 0:
                        front_tanh(m)
                    if j == 3:
                        front_dt(m, range(T))

                up(STEPS * b, between, after=after if m is not None else None)
                if m is not None:
                    front_ln(m, (0, 1))
                router_columns(b)
                if m is not None:
                    front_ln(m, (2, 3))
                    front_z(m)
                down(STEPS * b)

            def routed_step(step, m, half, off, count):
                up(step, lambda j: decays(m, half, off, count, j))
                down(step)

            act.dma_start(in_w[:], t["in_wT"].rearrange("(k p) e -> p k e", p=P)).then_inc(in_w_ld, 16)
            for dst, src in small:
                act.dma_start(dst, src).then_inc(const_ld, 16)
            act.wait_ge(const_ld, 16 * NCONST)
            act.activation(gate_tanh[:], gates[:], ACT.Tanh).then_inc(setup_a, 1)
            act.activation(neg_A[:], neg_A[:], ACT.Exp).then_inc(setup_a, 1)
            front_conv(0)
            for j in range(T):
                split_hi(0, 0, w1h, j)
            for et in range(T - 1):
                stage(1, et)
            front_tanh(0)
            stage(1, T - 1)
            act.wait_ge(setup_v, 3)
            front_yinit(0)
            front_xd(0)
            front_z(0)
            front_dt(0, range(T))
            act.wait_ge(setup_v, 3)
            front_ln(0, range(T))
            for n in range(2 * RING):
                for et in range(T):
                    decay(0, n, n % 2, et)
                if n == 1:
                    for et in range(T):
                        stage(2, et)
            for m in range(3, NB):
                for k in range(RING):
                    for et in range(T):
                        decay(0, RING * (m - 1) + k, k % 2, et)
                    stage(m, k)
            with act.Fori(NB - 1, DS // RING) as i:
                for k in range(RING):
                    for et in range(T):
                        decay(0, RING * i + k, k % 2, et)
            x_high(0)
            with act.Fori(0, NB - 1) as b:
                m = b + 1
                shared_step(b, m)

                def first_routed(j):
                    if j == 1:
                        router_exp(b)
                    decays(m, 0, 0, 1, j)

                up(STEPS * b + 1, first_routed)
                down(STEPS * b + 1)
                with act.Fori(0, 2) as q:
                    routed_step(STEPS * b + 2 * q + 2, m, 3 * q, 1, 3)
                    routed_step(STEPS * b + 2 * q + 3, m, 3 * q, 4, 3)
                routed_step(STEPS * b + NE - 1, m, DS // 2 - 2, 1, 3)
                up(STEPS * b + NE)
                x_high(m)
                act.wait_ge(acc_done, T * STEPS * (b + 1))
                act.dma_start(out[bass.ds(b, 1)].rearrange("a (i p) d -> p (a i) d", p=P), acc[:]).then_inc(out_st, 16)
            shared_step(NB - 1)
            router_exp(NB - 1)
            with act.Fori(1, NE) as e:
                up(STEPS * (NB - 1) + e)
                down(STEPS * (NB - 1) + e)
            up(STEPS * NB - 1, split=False)

        @block.vector
        def _(dve):
            def front_conv(m, taps=range(DC - 1), between=None):
                for k in taps:
                    back_ = DC - 1 - k
                    for et in range(T):
                        if k == 0:
                            dve.wait_ge(tap0_done, T * m + et + 1)
                        else:
                            dve.wait_ge(conv_done, T * (DC - 1) * m + T * (k - 1) + et + 1)
                        dve.scalar_tensor_tensor(out=u[:, et, back_:L], in0=conv_in(m, et)[:, 0:L - back_],
                                                 scalar=conv_w[:, et, k:k + 1], in1=u[:, et, back_:L],
                                                 op0=ALU.mult, op1=ALU.add).then_inc(conv_done, 1)
                        if between and k == 1:
                            between(et)

            def front_silu(m):
                for et in range(T):
                    dve.wait_ge(ut_done, T * m + et + 1)
                    dve.scalar_tensor_tensor(out=u[:, et, :], in0=dA[0][:, et, :], scalar=1.0, in1=u[:, et, :],
                                             op0=ALU.add, op1=ALU.mult).then_inc(u_ready, 1)

            def mean_and_var(m, stat_done, var_done):
                dve.wait_ge(stat_done, T * (m + 1))
                dve.memset(pause[:], 0.0)
                for i in range(T):
                    last = dve.bn_aggr(mv[:, i, :], bn[:, i, :])
                last.then_inc(mv_done, 1)
                dve.wait_ge(mv_done, 2 * m + (1 if stat_done is zstat else 2))
                dve.tensor_scalar(var_eps[:], mv[:, :, 1], EPS, None, ALU.add).then_inc(var_done, 1)

            def front_z_stats(m, tiles):
                dve.wait_ge(xz_ld, 16 * (m + 1))
                for i in tiles:
                    dve.bn_stats(bn[:, i, :], dA[1][:, i, :]).then_inc(zstat, 1)

            def front_zn(m):
                dve.wait_ge(zrstd, m + 1)
                for i in range(T):
                    dve.tensor_scalar(dA[1][:, i, :], dA[1][:, i, :], mv[:, i, 0:1], rstd[:, i:i + 1],
                                      ALU.subtract, ALU.mult).then_inc(zn_ready, 1)

            def front_z2(m):
                dve.wait_ge(zt_ready, m + 1)
                if some(m):
                    dve.wait_ge(acc_done, T * (STEPS * (m - 1) + 1))
                dve.scalar_tensor_tensor(out=z2[:], in0=st[1][:], scalar=1.0, in1=dA[1][:],
                                         op0=ALU.add, op1=ALU.mult).then_inc(z_ready, 1)

            def front_zero(m, odd):
                if odd:
                    dve.wait_ge(z_ready, m + 1)
                    dve.wait_ge(zero_done, 2 * m + 1)
                else:
                    dve.wait_ge(delta_ready, T * (m + 1))
                dve.memset(dA[odd][:, :, 0:1], 0.0).then_inc(zero_done, 1)

            def front_carry(m, tiles):
                if 0 in tiles:
                    if some(m):
                        dve.wait_ge(yadd_done, T * DS * m)
                    else:
                        dve.wait_ge(z_ready, 1)
                for et in tiles:
                    dve.wait_ge(e_ready, T * m + et + 1)
                    dve.tensor_scalar(st[1][:, et, :], dA[0][:, et, :], 1.0, None, ALU.add).then_inc(carry1, 1)
                for et in tiles:
                    dve.wait_ge(carry1, T * m + et + 1)
                    dve.scalar_tensor_tensor(out=st[1][:, et, :], in0=st[1][:, et, :], scalar=-1.0, in1=dA[0][:, et, :],
                                             op0=ALU.add, op1=ALU.subtract).then_inc(carry2, 1)
                for et in tiles:
                    dve.wait_ge(carry2, T * m + et + 1)
                    dve.wait_ge(dt_read, 2 * T * m + 2 * et + 2)
                    dve.tensor_tensor(delta[:, et, :], delta[:, et, :], st[1][:, et, :], ALU.subtract).then_inc(carry3, 1)

            def front_delta(m):
                for et in range(T):
                    dve.wait_ge(ln_ready, T * m + et + 1)
                    dve.wait_ge(carry3, T * m + et + 1)
                    dve.tensor_tensor(delta[:, et, :], delta[:, et, :], st[0][:, et, :], ALU.add).then_inc(delta_ready, 1)
                front_zero(m, 0)

            def front_du(m):
                dve.wait_ge(delta_ready, T * (m + 1))
                dve.wait_ge(yinit_done, T * (m + 1))
                dve.wait_ge(xp_done, m + 1)
                dve.scalar_tensor_tensor(out=u[:], in0=delta[:], scalar=0.5, in1=u[:],
                                         op0=ALU.mult, op1=ALU.mult).then_inc(du_ready, 1)

            def bmul(m, n, odd, turn):
                N = DS * m + n
                dve.wait_ge(bc_ld[odd], 16 * turn)
                dve.wait_ge(du_ready, m + 1)
                if some(N - 1):
                    dve.wait_ge(yadd_done, T * (N - 1))
                dve.tensor_tensor(st[odd][:], u[:], bc[odd][:, 0:1, :].broadcast_to([P, T, L]),
                                  ALU.mult).then_inc(bmul_done, 1)

            def scan(m, n, odd):
                N = DS * m + n
                dve.wait_ge(bmul_done, N + 1)
                dve.wait_ge(da_ready, T * (N + 1))
                flat = [v[odd][:].rearrange("p t l -> p (t l)") for v in (dA, st)]
                dve.tensor_tensor_scan(flat[1], flat[0], flat[1], 0.0, ALU.mult, ALU.add).then_inc(scan_done, 1)

            def cmul(m, n, odd):
                dve.wait_ge(scan_done, DS * m + n + 1)
                dve.tensor_tensor(st[odd][:], st[odd][:], bc[odd][:, 1:2, :].broadcast_to([P, T, L]),
                                  ALU.mult).then_inc(cmul_done, 1)

            def first_state(turn, k):
                n, odd = RING * turn + k, k % 2
                dve.wait_ge(bc_ld[k], 16 * (turn + 1))
                dve.wait_ge(du_ready, 1)
                if some(n - 1):
                    dve.wait_ge(hc_ready, T * (n - 1))
                dve.tensor_tensor(st[odd][:], u[:], first_bc[k][:, 0:1, :].broadcast_to([P, T, L]),
                                  ALU.mult).then_inc(bmul_done, 1)
                scan(0, n, odd)

            def states(m, half, off, count, k, places=T + 2):
                products(m, half, off, range(k * 3 * count // places, (k + 1) * 3 * count // places))

            def products(m, half, off, which):
                for q in which:
                    n, odd = off + q // 3, (off + q // 3) % 2
                    if q % 3 == 0:
                        bmul(m, 2 * half + n, odd, DS // RING + DS // 2 * (m - 1) + half + n // 2 + 1)
                    elif q % 3 == 1:
                        scan(m, 2 * half + n, odd)
                    else:
                        cmul(m, 2 * half + n, odd)

            def last_y_add(m):
                for et in range(T):
                    dve.wait_ge(yadd_done, T * DS * (m + 1) - T + et)
                    dve.wait_ge(cmul_done, DS * m)
                    dve.tensor_tensor(yacc[:, et, :], yacc[:, et, :], st[1][:, et, :], ALU.add).then_inc(yadd_done, 1)

            def first_make_y():
                dve.wait_ge(z_ready, 1)
                dve.wait_ge(xin_st, 16 * (NB - 1))
                for et in range(T):
                    dve.wait_ge(yadd_done, T * (DS - 1) + et + 1)
                    last = dve.scalar_tensor_tensor(out=yacc[:, et, :], in0=mid_ps[et][:], scalar=0.5, in1=z2[:, et, :],
                                                    op0=ALU.mult, op1=ALU.mult)
                last.then_inc(y_ready, 1)

            def make_y(m):
                dve.wait_ge(yadd_done, T * DS * (m + 1))
                dve.wait_ge(z_ready, m + 1)
                dve.scalar_tensor_tensor(out=yacc[:], in0=yacc[:], scalar=0.5, in1=z2[:],
                                         op0=ALU.mult, op1=ALU.mult).then_inc(y_ready, 1)

            def residual(m, tiles):
                dve.wait_ge(xres_ld, 16 * (m + 1))
                for i in tiles:
                    dve.wait_ge(yt_done, T * m + i + 1)
                    dve.scalar_tensor_tensor(out=x1[:, i, :], in0=front_ps[i][:], scalar=gate_tanh[:, 0:1],
                                             in1=x_rows[:, i, :], op0=ALU.mult, op1=ALU.add).then_inc(x1_ready, 1)
                for i in tiles:
                    dve.wait_ge(x1_ready, T * m + i + 1)
                    dve.bn_stats(bn[:, i, :], x1[:, i, :]).then_inc(x2stat, 1)

            def make_x2(m):
                dve.wait_ge(x2rstd, m + 1)
                for i in range(T):
                    dve.tensor_scalar(st[0][:, i, :], x1[:, i, :], mv[:, i, 0:1], rstd[:, i:i + 1],
                                      ALU.subtract, ALU.mult).then_inc(x2_ready, 1)

            def x_low(m):
                for i in range(T):
                    dve.wait_ge(xh_ready, T * m + i + 1)
                    cols = slice(i * P, (i + 1) * P)
                    dve.tensor_tensor(x_lo[:, :, cols], mid_ps[i][:].rearrange("p (k l) -> p k l", k=T),
                                      x_hi[:, :, cols].bitcast(F32), ALU.subtract).then_inc(xl_ready, 1)

            def router(m, part):
                links = 11
                first = 5
                done = [first if part else 0]

                def link(ins):
                    done[0] += 1
                    ins.then_inc(r_chain, 1)
                    dve.wait_ge(r_chain, links * m + done[0])

                def over(v):
                    return v.rearrange("p (t a) -> p t a", a=1).broadcast_to([P, T, NE])

                ps = ps_m[:, 0:8 * T].rearrange("p (i e) -> p i e", e=8)[:, :, 0:NE]
                gb = gate_b[:].rearrange("p (a e) -> p a e", a=1).broadcast_to([P, T, NE])
                bb = biases[:].rearrange("p (a e) -> p a e", a=1).broadcast_to([P, T, NE])
                if part == 0:
                    dve.wait_ge(gl_done, m + 1)
                    dve.tensor_tensor(logits[:], ps, gb, ALU.add).then_inc(logit_read, 1)
                    dve.wait_ge(logit_read, m + 1)
                    link(dve.tensor_reduce(lmax[:], logits[:], AX_X, ALU.max))
                    dve.tensor_tensor(logits[:], logits[:], over(lmax[:]), ALU.subtract).then_inc(r_sub, 1)
                    dve.wait_ge(r_exp, m + 1)
                    link(dve.tensor_reduce(psum_[:], probs[:], AX_X, ALU.add))
                    link(dve.reciprocal(psum_[:], psum_[:]))
                    link(dve.tensor_tensor(probs[:], probs[:], over(psum_[:]), ALU.mult))
                    link(dve.tensor_tensor(biased[:], probs[:], bb, ALU.add))
                    assert done[0] == first
                    return
                mine = biased[:].rearrange("p t (e a) -> p t e a", a=1).broadcast_to([P, T, NE, NE])
                other = biased[:].rearrange("p t (a e) -> p t a e", a=1).broadcast_to([P, T, NE, NE])
                tie = earlier[:].rearrange("p (a e) f -> p a e f", a=1).broadcast_to([P, T, NE, NE])
                for i in range(T):
                    dve.tensor_tensor(eq[:, i], other[:, i], mine[:, i], ALU.is_equal)
                    last = dve.tensor_tensor(gt[:, i], other[:, i], mine[:, i], ALU.is_gt)
                link(last)
                for i in range(T):
                    last = dve.tensor_tensor(eq[:, i], eq[:, i], tie[:, i], ALU.mult)
                link(last)
                link(dve.tensor_tensor(gt, gt, eq, ALU.add))
                link(dve.tensor_reduce(rank[:], gt, AX_X, ALU.add))
                link(dve.scalar_tensor_tensor(out=coef[:], in0=rank[:], scalar=float(TOP_K), in1=probs[:],
                                              op0=ALU.is_lt, op1=ALU.mult))
                link(dve.tensor_reduce(psum_[:], coef[:], AX_X, ALU.add))
                dve.reciprocal(psum_[:], psum_[:]).then_inc(coef_ready, 1)
                dve.wait_ge(coef_ready, 2 * m + 1)
                dve.scalar_tensor_tensor(out=coef[:], in0=coef[:], scalar=half_tgf[:, 0:1], in1=over(psum_[:]),
                                         op0=ALU.mult, op1=ALU.mult).then_inc(coef_ready, 1)
                dve.wait_ge(coef_ready, 2 * m + 2)
                assert done[0] == links

            def split_lo(step, j):
                dve.wait_ge(w1h, T * step + j + 1)
                cols = slice(j * P, (j + 1) * P)
                dve.tensor_tensor(w_lo[0][:, :, cols], w_raw[0][:, :, cols], w_hi[0][:, :, cols].bitcast(F32),
                                  ALU.subtract).then_inc(w1l, 1)

            def step_(step, e, between=None, split=True):
                def add_out(i):
                    dve.wait_ge(y_done, T * step + i + 1)
                    if e is None:
                        scale, before = half_tgf[:, 0:1], x1
                    else:
                        dve.wait_ge(acc_done, T * step + i)
                        scale, before = coef[:, i, bass.ds(e, 1)], acc
                    dve.scalar_tensor_tensor(out=acc[:, i, :], in0=ps_y[i % 3][:], scalar=scale, in1=before[:, i, :],
                                             op0=ALU.mult, op1=ALU.add).then_inc(acc_done, 1)

                for j in range(T):
                    dve.wait_ge(t_done, T * step + j + 1)
                    dve.scalar_tensor_tensor(out=h_tmp[j % 2][:], in0=h_tmp[j % 2][:], scalar=1.0, in1=ps_h1[j % 2][:],
                                             op0=ALU.add, op1=ALU.mult).then_inc(m_done, 1)
                    if split:
                        split_lo(step + 1, j)
                    dve.wait_ge(m_done, T * step + j + 1)
                    dve.wait_ge(hg_done, T * step + j + 1)
                    dve.tensor_tensor(h_tmp[j % 2][:], h_tmp[j % 2][:], ps_hg[j % 2][:], ALU.mult).then_inc(h_made, 1)
                    if between:
                        between(j)
                add_out(0)
                add_out(1)
                if between:
                    between(T)
                add_out(2)
                add_out(3)
                if between:
                    between(T + 1)

            dve.memset(ones[:], 1.0)
            dve.memset(gw_hi[:].bitcast(F32), 0.0)
            dve.memset(gw_lo[:].bitcast(F32), 0.0)
            dve.memset(minus_half[:], -0.5).then_inc(setup_v, 1)
            dve.wait_ge(const_ld, 16 * NCONST)
            dve.wait_ge(setup_v, 1)
            dve.wait_ge(warm, WARM_START)
            dve.tensor_scalar(xproj_w[:], xproj_w[:], 0.5, None, ALU.mult).then_inc(setup_v, 1)
            dve.tensor_scalar(half_D[:], half_D[:], 0.5, None, ALU.mult).then_inc(setup_v, 1)
            dve.tensor_copy(gw_hi[:, :, 0:NE], gw_raw[:]).then_inc(setup_v, 1)
            dve.wait_ge(setup_v, 4)
            dve.tensor_tensor(gw_lo[:, :, 0:NE], gw_raw[:], gw_hi[:, :, 0:NE].bitcast(F32), ALU.subtract).then_inc(setup_v, 1)
            dve.wait_ge(setup_a, 2)
            dve.tensor_scalar(half_tgf[:], gate_tanh[:, 1:2], 0.5, None, ALU.mult).then_inc(setup_v, 1)
            dve.tensor_scalar(neg_A[:], neg_A[:], -1.0, None, ALU.mult).then_inc(setup_v, 1)
            dve.wait_ge(setup_v, 7)
            front_conv(0, between=lambda q: q > 0 and front_z_stats(0, {1: (0,), 2: (1,), 3: (2, 3)}[q]))
            mean_and_var(0, zstat, zvar)
            front_silu(0)
            front_zn(0)
            front_z2(0)
            front_carry(0, (0, 1))
            front_carry(0, (2, 3))
            front_delta(0)
            front_du(0)
            front_zero(0, 1)
            for k in range(RING):
                first_state(0, k)
            with dve.Fori(1, DS // RING - 1) as i:
                for k in range(RING):
                    first_state(i, k)
            for k in range(RING):
                first_state(DS // RING - 1, k)
            dve.wait_ge(scan_done, DS)
            for et in range(T):
                dve.tensor_tensor(st[1][:, et, :], st[1][:, et, :], first_bc[RING - 1][:, 1, :],
                                  ALU.mult).then_inc(last_hc_ready, 1)
            first_make_y()
            residual(0, range(T))
            mean_and_var(0, x2stat, x2var)
            make_x2(0)
            x_low(0)
            with dve.Fori(0, NB - 1) as b:
                m = b + 1
                front_conv(m, range(DC - 2))

                def front(k):
                    if k == 0:
                        front_conv(m, (DC - 2,))
                        front_silu(m)
                    if k == 1:
                        front_z_stats(m, range(T))
                        mean_and_var(m, zstat, zvar)
                    if k == 2:
                        front_zn(m)
                    if k == 3:
                        front_carry(m, (0, 1))
                    if k == T:
                        front_carry(m, (2, 3))
                        front_delta(m)
                        front_du(m)

                def first_routed(k):
                    if k == 0:
                        front_z2(m)
                        front_zero(m, 1)
                    if k == 1:
                        router(b, 0)
                    if k == 2:
                        router(b, 1)
                    products(m, 0, 0, ((), (), (), (0,), (1,), (2,))[k])

                def last(k):
                    if k == 1:
                        residual(m, (0, 1))
                    if k == 2:
                        residual(m, (2, 3))
                        mean_and_var(m, x2stat, x2var)
                    if k == 3:
                        make_x2(m)
                    if k == T:
                        x_low(m)

                step_(STEPS * b, None, front)
                step_(STEPS * b + 1, 0, first_routed)
                with dve.Fori(0, 2) as q:
                    step_(STEPS * b + 2 * q + 2, 2 * q + 1, lambda k: states(m, 3 * q, 1, 3, k))
                    step_(STEPS * b + 2 * q + 3, 2 * q + 2, lambda k: states(m, 3 * q, 4, 3, k))
                step_(STEPS * b + NE - 1, NE - 2, lambda k: states(m, DS // 2 - 2, 1, 3, k))
                last_y_add(m)
                make_y(m)
                step_(STEPS * b + NE, NE - 1, last)
            step_(STEPS * (NB - 1), None)
            router(NB - 1, 0)
            router(NB - 1, 1)
            with dve.Fori(0, NE - 1) as e:
                step_(STEPS * (NB - 1) + e + 1, e)
            step_(STEPS * NB - 1, NE - 1, split=False)

        @block.gpsimd
        def _(pool):
            def power(sem_var, sem_rstd, m):
                pool.wait_ge(sem_var, m + 1)
                pool.tensor_tensor(rstd[:], var_eps[:], minus_half[:], ALU.pow).then_inc(sem_rstd, 1)

            def y_add(m, n, odd, tiles=range(T)):
                N = DS * m + n
                pool.wait_ge(yinit_done, T * (m + 1))
                pool.wait_ge(cmul_done, DS * (m - 1) + n + 1)
                for et in tiles:
                    if some(T * N + et - T + 1):
                        pool.wait_ge(yadd_done, T * N + et - T + 1)
                    pool.tensor_tensor(yacc[:, et, :], yacc[:, et, :], st[odd][:, et, :], ALU.add).then_inc(yadd_done, 1)

            def h_low(step, j):
                pool.wait_ge(hh_ready, T * step + j + 1)
                pool.tensor_tensor(h_lo[:, j, :], h_tmp[j % 2][:], h_hi[:, j, :].bitcast(F32),
                                   ALU.subtract).then_inc(hl_ready, 1)

            def split_gate(step, j):
                pool.wait_ge(wgh, T * step + j + 1)
                cols = slice(j * P, (j + 1) * P)
                pool.tensor_tensor(w_lo[1][:, :, cols], w_raw[1][:, :, cols], w_hi[1][:, :, cols].bitcast(F32),
                                   ALU.subtract).then_inc(wgl, 1)

            def split_down(step, tiles=range(T)):
                for j in tiles:
                    pool.wait_ge(w2h, T * step + j + 1)
                    pool.tensor_tensor(w_lo[2][:, j], w_raw[2][:, j], w_hi[2][:, j].bitcast(F32),
                                       ALU.subtract).then_inc(w2l, 1)

            def plain_step(step):
                for j in range(T):
                    h_low(step, j)
                    split_gate(step + 1, j)
                split_down(step + 1)

            def shared_step(b, m=None):
                for j in range(T):
                    h_low(STEPS * b, j)
                    if j < 2:
                        split_down(STEPS * b, (2 * j, 2 * j + 1))
                    split_gate(STEPS * b + 1, j)
                    if j == 1 and m is not None:
                        power(zvar, zrstd, m)
                split_down(STEPS * b + 1)

            def last_step(b, m):
                for j in range(T):
                    if j == 3:
                        power(x2var, x2rstd, m)
                    h_low(STEPS * b + NE, j)
                    split_gate(STEPS * (b + 1), j)

            def one_state(step, m, n, odd):
                for j in range(T):
                    h_low(step, j)
                    split_gate(step + 1, j)
                split_down(step + 1)
                y_add(m, n, odd)

            def three_states(step, m, n, odd, last=False):
                for j in range(T):
                    h_low(step, j)
                    if j == 2:
                        y_add(m, n, odd, (0, 1))
                    if j == 3:
                        y_add(m, n, odd, (2, 3))
                    split_gate(step + 1, j)
                y_add(m, n + 1, 1 - odd)
                split_down(step + 1)
                if not last:
                    y_add(m, n + 2, odd)

            def part_of(w, j):
                return (slice(None), slice(None), slice(j * P, (j + 1) * P)) if w < 2 else (slice(None), j)

            def first_high(w, hi):
                pool.wait_ge(raw_ld[w], 16)
                for j in range(T):
                    pool.tensor_copy(w_hi[w][part_of(w, j)], w_raw[w][part_of(w, j)]).then_inc(hi, 1)

            def first_low(w, hi, lo):
                for j in range(T):
                    sel = part_of(w, j)
                    pool.wait_ge(hi, j + 1)
                    pool.tensor_tensor(w_lo[w][sel], w_raw[w][sel], w_hi[w][sel].bitcast(F32), ALU.subtract).then_inc(lo, 1)

            def first_products(turn, k):
                n = RING * turn + k
                pool.wait_ge(scan_done, n + 1)
                for et in range(T):
                    if some(T * n + et - T + 1):
                        pool.wait_ge(yadd_done, T * n + et - T + 1)
                    ins = pool.tensor_tensor(first_hc[:, et, :], st[k % 2][:, et, :], first_bc[k][:, 1, :], ALU.mult)
                    ins.then_inc(hc_ready, 1)

            pool.wait_ge(setup_v, 1)
            first_low(0, w1h, w1l)
            power(zvar, zrstd, 0)
            first_high(1, wgh)
            first_low(1, wgh, wgl)
            for k in range(RING):
                first_products(0, k)
            with pool.Fori(1, DS // RING - 1) as i:
                for k in range(RING):
                    first_products(i, k)
            for k in range(RING - 1):
                first_products(DS // RING - 1, k)
            power(x2var, x2rstd, 0)
            with pool.Fori(0, NB - 1) as b:
                m = b + 1
                shared_step(b, m)
                one_state(STEPS * b + 1, m, 0, 0)
                with pool.Fori(0, 2) as q:
                    three_states(STEPS * b + 2 * q + 2, m, 6 * q + 1, 1)
                    three_states(STEPS * b + 2 * q + 3, m, 6 * q + 4, 0)
                three_states(STEPS * b + NE - 1, m, DS - 3, 1, last=True)
                last_step(b, m)
                pool.wait_ge(out_st, 16 * (b + 1))
            shared_step(NB - 1)
            with pool.Fori(1, NE) as e:
                plain_step(STEPS * (NB - 1) + e)
            for j in range(T):
                h_low(STEPS * NB - 1, j)


def kernel(**inputs):
    import numpy as np
    import concourse.bacc as bacc
    from concourse.bass_utils import run_bass_kernel_spmd

    g = {k.replace("L0_xattn_", "").replace("L0_ffn_", ""): np.asarray(v) for k, v in inputs.items()}
    ne = g["W1"].shape[0]

    def columns(v):
        return v.reshape(-1, P).T

    arrays = {
        "x": g["x"], "ctxT": g["ctx_1024"].transpose(0, 2, 1), "g_xattn": g["g_xattn"], "g_ffn": g["g_ffn"],
        "in_wT": g["in_proj_w"].T, "conv_w": g["conv_w"], "conv_b": columns(g["conv_b"]), "xproj_wT": g["x_proj_w"].T,
        "dt_wT": g["dt_proj_w"].T, "dt_b": columns(g["dt_proj_b"]), "A_log": g["A_log"], "D": columns(g["D"]),
        "W1": g["W1"], "Wg": g["Wg"], "W2": g["W2"], "Ws1": g["Ws1"], "Wsg": g["Wsg"], "Ws2": g["Ws2"],
        "gate_w": g["gate_w"], "gate_b": g["gate_b"], "biases": g["biases"],
        "ident": np.eye(P, dtype=np.float32), "earlier": np.tril(np.ones((ne, ne), np.float32), -1).reshape(-1),
    }
    nc = bacc.Bacc("TRN2", target_bir_lowering=False, num_devices=1)
    fed, args = {}, {}
    for name in NAMES:
        a = np.ascontiguousarray(arrays[name])
        fed[f"in_{name}_dram"] = a
        args[name] = nc.dram_tensor(f"in_{name}_dram", a.shape, mybir.dt.from_np(a.dtype), kind="ExternalInput").ap()
    out = nc.dram_tensor("out_dram", g["x"].shape, F32, kind="ExternalOutput").ap()
    gated_block(nc, args, out)
    return run_bass_kernel_spmd(nc, [fed], core_ids=[0]).results[0]["out_dram"]
```
